# Optimizing a Trainium2 kernel written in Bass

```python
import numpy as np
import jax
import jax.numpy as jnp

def _softmax(x, axis=-1):
    return jax.nn.softmax(x, axis=axis)

def _gelu(x):
    return jax.nn.gelu(x, approximate=True)

def _silu(x):
    return jax.nn.silu(x)

def _sigmoid(x):
    return jax.nn.sigmoid(x)

def _layernorm(x, axis=-1, eps=1e-05):
    m = jnp.mean(x, axis=axis, keepdims=True)
    v = jnp.var(x, axis=axis, keepdims=True)
    return (x - m) / jnp.sqrt(v + eps)

def _scatter_add(tgt, idx, src, axis=0):
    return tgt.at[idx].add(src)

def _segment_sum(src, seg, n):
    return jax.ops.segment_sum(src, seg, n)
kernel_name = 'mk_prb_d1_jaxref_r4_2107a5'

def setup_inputs(seed: int=0):
    np.random.seed(seed)
    _w = jnp.asarray

    def _L0_attn_setup():
        import jax, jax.numpy as jnp
        import numpy as np
        DIM = 256
        HEADS = 16
        HEAD_DIM = DIM // HEADS
        DECAY = 0.95
        EPS = 1e-05

        def _decay_mask(S, dtype):
            idx = jnp.arange(S)
            diff = (idx[:, None] - idx[None, :]).astype(jnp.float32)
            mask = jnp.where(diff >= 0, jnp.exp(diff * np.log(DECAY)), 0.0)
            return mask.astype(dtype)
        key = jax.random.key(seed)
        ks = jax.random.split(key, 11)
        B, S, D = (2, 512, DIM)
        s = 1.0 / np.sqrt(D)
        inp = {'x': jax.random.normal(ks[0], (B, S, D), dtype=jnp.float32), 'Wq': jax.random.normal(ks[1], (D, D), dtype=jnp.float32) * s, 'bq': jnp.zeros((D,), jnp.float32), 'Wk': jax.random.normal(ks[2], (D, D), dtype=jnp.float32) * s, 'bk': jnp.zeros((D,), jnp.float32), 'Wv': jax.random.normal(ks[3], (D, D), dtype=jnp.float32) * s, 'bv': jnp.zeros((D,), jnp.float32), 'Wo': jax.random.normal(ks[4], (D, D), dtype=jnp.float32) * s, 'bo': jnp.zeros((D,), jnp.float32), 'gamma': jnp.ones((D,), jnp.float32), 'beta': jnp.zeros((D,), jnp.float32)}
        return inp
    _L0_attn_in = _L0_attn_setup()

    def _L0_ffn_setup():
        import jax, jax.numpy as jnp
        import numpy as np
        NUM_EXPERTS = 8
        EXPERT_CAPACITY = 2.0
        key = jax.random.key(seed)
        k1, k2, k3, k4 = jax.random.split(key, 4)
        B, T, C, H, E = (4, 1024, 256, 1024, NUM_EXPERTS)
        x = jax.random.normal(k1, (B, T, C), jnp.float32)
        gate_w = jax.random.normal(k2, (C, E), jnp.float32) * 0.02
        w1 = jax.random.normal(k3, (E, C, H), jnp.float32) * 0.02
        w2 = jax.random.normal(k4, (E, H, C), jnp.float32) * 0.02
        return {'x': x, 'gate_w': gate_w, 'w1': w1, 'w2': w2}
    _L0_ffn_in = _L0_ffn_setup()
    _d = {'L0_attn_x': _L0_attn_in['x'], 'L0_attn_Wq': _L0_attn_in['Wq'], 'L0_attn_bq': _L0_attn_in['bq'], 'L0_attn_Wk': _L0_attn_in['Wk'], 'L0_attn_bk': _L0_attn_in['bk'], 'L0_attn_Wv': _L0_attn_in['Wv'], 'L0_attn_bv': _L0_attn_in['bv'], 'L0_attn_Wo': _L0_attn_in['Wo'], 'L0_attn_bo': _L0_attn_in['bo'], 'L0_attn_gamma': _L0_attn_in['gamma'], 'L0_attn_beta': _L0_attn_in['beta'], 'L0_ffn_gate_w': _L0_ffn_in['gate_w'], 'L0_ffn_w1': _L0_ffn_in['w1'], 'L0_ffn_w2': _L0_ffn_in['w2']}
    _x0 = _d['L0_attn_x']
    _d['L0_attn_x'] = jax.random.normal(jax.random.fold_in(jax.random.key(seed), 1), (32, 512, 256), dtype=_x0.dtype)
    del _x0
    return _d

def reference(L0_attn_x, L0_attn_Wq, L0_attn_bq, L0_attn_Wk, L0_attn_bk, L0_attn_Wv, L0_attn_bv, L0_attn_Wo, L0_attn_bo, L0_attn_gamma, L0_attn_beta, L0_ffn_gate_w, L0_ffn_w1, L0_ffn_w2):

    def _L0_attn_ref(x, Wq, bq, Wk, bk, Wv, bv, Wo, bo, gamma, beta):
        import jax, jax.numpy as jnp
        import numpy as np
        DIM = 256
        HEADS = 16
        HEAD_DIM = DIM // HEADS
        DECAY = 0.95
        EPS = 1e-05

        def _decay_mask(S, dtype):
            idx = jnp.arange(S)
            diff = (idx[:, None] - idx[None, :]).astype(jnp.float32)
            mask = jnp.where(diff >= 0, jnp.exp(diff * np.log(DECAY)), 0.0)
            return mask.astype(dtype)
        B, S, D = x.shape
        H, hd = (HEADS, HEAD_DIM)

        def split_heads(y):
            return y.reshape(B, S, H, hd).transpose(0, 2, 1, 3)
        q = split_heads(x @ Wq + bq)
        k = split_heads(x @ Wk + bk)
        v = split_heads(x @ Wv + bv)
        mask = _decay_mask(S, x.dtype)
        scores = jnp.einsum('bhid,bhjd->bhij', q, k) * mask
        out = jnp.einsum('bhij,bhjd->bhid', scores, v)
        out = out.transpose(0, 2, 1, 3).reshape(B, S, D)
        out = out @ Wo + bo
        y = out.transpose(0, 2, 1)
        yg = y.reshape(B, H, hd, S)
        mu = yg.mean(axis=(2, 3), keepdims=True)
        var = yg.var(axis=(2, 3), keepdims=True)
        yn = (yg - mu) / jnp.sqrt(var + EPS)
        yn = yn.reshape(B, D, S) * gamma[None, :, None] + beta[None, :, None]
        return yn.transpose(0, 2, 1)

    def _L0_ffn_ref(x, gate_w, w1, w2):
        import jax, jax.numpy as jnp
        import numpy as np
        NUM_EXPERTS = 8
        EXPERT_CAPACITY = 2.0
        B, T, C = x.shape
        E = gate_w.shape[1]
        cap = int(EXPERT_CAPACITY * T / E)
        scores = jnp.einsum('BTC,CE->BTE', x, gate_w)
        probs = jax.nn.softmax(scores, axis=-1)
        probs_et = jnp.transpose(probs, (0, 2, 1))
        top_p, top_idx = jax.lax.top_k(probs_et, cap)
        xin = jnp.take_along_axis(x[:, None, :, :], top_idx[..., None], axis=2)
        h = jax.nn.gelu(jnp.einsum('BElC,ECH->BElH', xin, w1), approximate=False)
        y = jnp.einsum('BElH,EHC->BElC', h, w2)
        y = y * top_p[..., None]
        b_idx = jnp.arange(B)[:, None, None]
        out = jnp.zeros((B, T, C), x.dtype).at[b_idx, top_idx].add(y)
        return out
    x = L0_attn_x
    xn = _layernorm(x, axis=-1)
    x = x + _L0_attn_ref(xn, L0_attn_Wq, L0_attn_bq, L0_attn_Wk, L0_attn_bk, L0_attn_Wv, L0_attn_bv, L0_attn_Wo, L0_attn_bo, L0_attn_gamma, L0_attn_beta) + _L0_ffn_ref(xn, L0_ffn_gate_w, L0_ffn_w1, L0_ffn_w2)
    return x

_drawn_inputs = setup_inputs


def setup_inputs(seed=0):
    import zlib

    import numpy as np

    out = dict(_drawn_inputs(seed))
    spreads = {'L0_attn_bq': (0.0, 0.1),
     'L0_attn_bk': (0.0, 0.1),
     'L0_attn_bv': (0.0, 0.1),
     'L0_attn_bo': (0.0, 0.8),
     'L0_attn_gamma': (1.0, 0.2),
     'L0_attn_beta': (0.0, 0.1)}
    factors = {'L0_ffn_gate_w': 3.37, 'L0_ffn_w1': 2.975, 'L0_ffn_w2': 2.904}
    for name, (base, spread) in spreads.items():
        noise = np.random.default_rng([zlib.crc32(name.encode()), seed]).standard_normal(out[name].shape)
        drawn = base * np.exp(spread * noise) if base else spread * noise
        out[name] = jnp.asarray(drawn.astype(out[name].dtype))
    for name, factor in factors.items():
        out[name] = (out[name] * factor).astype(out[name].dtype)
    return out
```

```python
from contextlib import ExitStack

import concourse.bass as bass
from concourse import mybir

F32 = mybir.dt.float32
F32R = mybir.dt.float32r
I32 = mybir.dt.int32
U32 = mybir.dt.uint32
ALU = mybir.AluOpType
ACT = mybir.ActivationFunctionType
AX = mybir.AxisListType

P = 128
B, S, D = 32, 512, 256
HEADS, HD = 16, 16
E, FF = 8, 1024
CAP = 2 * S // E
DH = D // P
TT = S // P
FT = FF // P
PAIRS = P // (2 * HD)
DECAY = 0.95
EPS = 1e-5
MAGIC = 1597463007.0
NEWTON = 3
RS = 2 + 4 * NEWTON
GRP = 4
NG = B // GRP
BE = B * E
C_ID, C_MASK, C_G, C_BD, C_QD, C_PAR, C_KD, C_OFF, C_N = 0, 128, 256, 384, 512, 640, 642, 643, 645
V_BQ, V_BK, V_BO, V_GA, V_BE, V_N = 0, 2, 4, 6, 8, 10


def wait_apart(eng, sem, value, passed):
    eng.wait_ge(sem, value)
    if not isinstance(value, int):
        eng.sem_inc(passed, 1)


def rsqrt_steps(eng, var, ve, r, a, chain, base, passed):
    k = 0

    def step(ins):
        nonlocal k
        k += 1
        ins.then_inc(chain, 1)
        wait_apart(eng, chain, base + k, passed)

    step(eng.tensor_scalar(ve, var, EPS, None, ALU.add))
    step(eng.tensor_scalar(r.bitcast(I32), ve.bitcast(I32), -0.5, MAGIC, ALU.mult, ALU.add))
    for _ in range(NEWTON):
        step(eng.tensor_tensor(a, r, r, ALU.mult))
        step(eng.tensor_tensor(a, a, ve, ALU.mult))
        step(eng.tensor_scalar(a, a, -0.5, 1.5, ALU.mult, ALU.add))
        step(eng.tensor_tensor(r, r, a, ALU.mult))


def attention_block(nc, x, xn_d, out, wq, wk, wv, wo, gw, bvr, cst_d, vec_d, cst, vec, gsc):
    with ExitStack() as ctx:
        def sb(name, shape, dt=F32):
            return ctx.enter_context(nc.sbuf_tensor(name, shape, dt))

        def ps(name):
            return ctx.enter_context(nc.psum_tensor(name, [P, 512], F32))

        def sem(name):
            return ctx.enter_context(nc.semaphore(name))

        VG = D + 2 * E
        wst = sb("wst", [P, 4, DH, D])
        gst_w = sb("gate_stage", [P, DH, E])
        bv = sb("bv_rows", [P, D])
        w_hi = [sb(f"w_hi{i}", [P, DH, D], F32R) for i in range(4)]
        w_lo = [sb(f"w_lo{i}", [P, DH, D], F32R) for i in range(4)]
        vg_hi = sb("vg_hi", [P, DH, VG], F32R)
        xb = [sb(f"x{i}", [P, TT, D]) for i in range(2)]
        xn = sb("xn", [P, TT, D])
        st = sb("ln_stats", [P, TT, 6])
        mv = sb("ln_mv", [P, TT, 2])
        ln_ve, ln_r, ln_a = (sb(f"ln_{n}", [P, TT]) for n in ("ve", "r", "a"))
        x_hi = sb("x_hi", [P, DH, S], F32R)
        x_lo = sb("x_lo", [P, DH, S], F32R)
        q32 = sb("q32", [P, DH, S])
        k32 = sb("k32", [P, DH, S])
        q_hi = sb("q_hi", [P, DH, 2, S], F32R)
        q_lo = sb("q_lo", [P, DH, 2, S], F32R)
        k_hi = sb("k_hi", [P, DH, S], F32R)
        k_lo = sb("k_lo", [P, DH, S], F32R)
        qd = sb("q_decayed", [P, DH, S])
        kn = sb("k_natural", [P, TT - 1, D])
        v = sb("v", [P, TT, D])
        vm = sb("v_parity", [P, TT, 2, D])
        s_sb = [sb(f"s_sb{i}", [P, DH, 2, P]) for i in range(4)]
        kvt = sb("kv_masked", [P, DH, P])
        state = [sb(f"state{i}", [P, DH, P]) for i in range(TT - 1)]
        a_hi = sb("a_hi", [P, DH, S], F32R)
        a_lo = sb("a_lo", [P, DH, S], F32R)
        o32 = sb("o32", [P, DH, S])
        ost = sb("o_stats", [P, DH, 6])
        gm = sb("g_moments", [P, DH, 2])
        gs = sb("g_means", [P, DH, 2])
        gn_ve, gn_r, gn_a, gn_m, gn_s, gn_b = (sb(f"gn_{n}", [P, DH]) for n in ("ve", "r", "a", "m", "s", "b"))
        yT = sb("yT", [P, DH, S])
        res = sb("res", [P, TT, D])

        fb = [ps("front0"), ps("front1")]
        sbk = [ps("scores0"), ps("scores1")]
        cb = [ps("misc0"), ps("misc1")]
        ob = [ps("attn0"), ps("attn1")]

        pool_passed = sem("pool_passed")
        dve_passed = sem("dve_passed")
        consts_in = sem("consts_in")
        w_split = sem("w_split")
        vm_zero = sem("vm_zero")
        x_in = [sem("x_in0"), sem("x_in1")]
        ln_st = sem("ln_st")
        ln_mv = sem("ln_mv_ready")
        ln_chain = sem("ln_chain")
        xn_ready = sem("xn_ready")
        xn_stored = sem("xn_stored")
        xnt_ready = sem("xnt_ready")
        xhi_ready = sem("xhi_ready")
        xlo_ready = sem("xlo_ready")
        qk_mm = sem("qk_mm")
        qk32 = sem("qk32_ready")
        qk_hi = sem("qk_hi_ready")
        qk_lo = sem("qk_lo_ready")
        qd_ready = sem("qd_ready")
        v_mm = sem("v_mm")
        v_ready = sem("v_ready")
        v_out = sem("v_bank_read")
        vm_ready = sem("vm_ready")
        kt_ready = sem("kt_ready")
        kn_ready = sem("kn_ready")
        kv_ready = sem("kv_ready")
        kv_read = sem("kv_read")
        st_ready = sem("state_ready")
        s_mm = sem("s_mm")
        s_ready = sem("s_ready")
        av_done = sem("av_done")
        ahi_ready = sem("ahi_ready")
        alo_ready = sem("alo_ready")
        wo_mm = sem("wo_mm")
        o_ready = sem("o_ready")
        ost_ready = sem("ost_ready")
        omv_ready = sem("omv_ready")
        gm_ready = sem("gm_ready")
        gst_mm = sem("gst_mm")
        gs_ready = sem("gs_ready")
        gn_chain = sem("gn_chain")
        gn_ready = sem("gn_ready")
        y_ready = sem("y_ready")
        yt_mm = sem("yt_mm")
        res_ready = sem("res_ready")
        out_stored = sem("out_stored")

        ident = cst[:, C_ID:C_ID + P]
        mask = cst[:, C_MASK:C_MASK + P]
        gones = cst[:, C_G:C_G + P]
        bdm = cst[:, C_BD:C_BD + P]
        qdec = cst[:, C_QD:C_QD + P]

        def parity(p):
            return cst[:, C_PAR + p:C_PAR + p + 1]

        kdec = cst[:, C_KD:C_KD + 1]

        def repeat(ap, n):
            return ap.unsqueeze(1).broadcast_to([P, n, ap.shape[1]])

        x_v = x.rearrange("b (t p) c -> b p t c", p=P)
        xn_v = xn_d.rearrange("(b t p) c -> b p t c", p=P, t=TT)
        out_v = out.rearrange("b (t p) c -> b p t c", p=P)

        def batches(eng, front, core):
            front(0, 0, 0)
            core(0, 0, 0, lambda part=None: front(1, 0, 1, part))
            core(1, 0, 1, lambda part=None: front(2, 1, 0, part))
            with eng.Fori(1, B // 2 - 1) as i:
                core(2 * i, i, 0, lambda part=None: front(2 * i + 1, i, 1, part))
                core(2 * i + 1, i, 1, lambda part=None: front(2 * i + 2, i + 1, 0, part))
            core(B - 2, B // 2 - 1, 0, lambda part=None: front(B - 1, B // 2 - 1, 1, part))
            core(B - 1, B // 2 - 1, 1, lambda part=None: None)

        block = ctx.enter_context(nc.Block())

        @block.sync
        def _(sp):
            sp.dma_start(cst[:], cst_d).then_inc(consts_in, 16)
            sp.dma_start(vec[:], vec_d).then_inc(consts_in, 16)
            sp.dma_start(bv[:], bvr).then_inc(consts_in, 16)
            for i, w in enumerate((wq, wk, wv, wo)):
                sp.dma_start(wst[:, i], w.rearrange("(h p) n -> p h n", p=P)).then_inc(consts_in, 16)
            sp.dma_start(gst_w[:], gw.rearrange("(h p) n -> p h n", p=P)).then_inc(consts_in, 16)
            sp.dma_start(xb[0][:], x_v[0]).then_inc(x_in[0], 16)
            sp.dma_start(xb[1][:], x_v[1]).then_inc(x_in[1], 16)

            def front(b, k, par, part=None):
                sp.wait_ge(xn_ready, TT * b + TT)
                sp.dma_start(xn_v[b], xn[:]).then_inc(xn_stored, 16)

            def core(b, k, par, nxt, last=False):
                nxt()
                sp.wait_ge(res_ready, 2 * b + 2)
                sp.dma_start(out_v[b], res[:]).then_inc(out_stored, 16)
                if not isinstance(b, int) or b < B - 2:
                    sp.dma_start(xb[par][:], x_v[b + 2]).then_inc(x_in[par], 16)

            batches(sp, front, core)
            sp.wait_ge(xn_stored, 16 * B)
            sp.wait_ge(out_stored, 16 * B)

        @block.gpsimd
        def _(pool):
            pool.memset(vm[:], 0.0).then_inc(vm_zero, 1)
            pool.wait_ge(consts_in, 16 * 8)
            pool.wait_ge(vm_zero, 1)

            def front(b, k, par, part=None):
                wait_apart(pool, ln_mv, TT * b + TT, pool_passed)
                rsqrt_steps(pool, mv[:, :, 1], ln_ve[:], ln_r[:], ln_a[:], ln_chain, RS * b,
                            pool_passed)
                wait_apart(pool, xn_stored, 16 * b, pool_passed)
                wait_apart(pool, xnt_ready, 2 * b, pool_passed)
                for t in range(TT):
                    pool.tensor_scalar(xn[:, t, :], xb[par][:, t, :], mv[:, t, 0:1], ln_r[:, t:t + 1],
                                       ALU.subtract, ALU.mult).then_inc(xn_ready, 1)
                pool.wait_ge(av_done, 16 * b)
                for h in range(DH):
                    pool.wait_ge(qk32, 4 * b + h + 1)
                    pool.tensor_tensor(qd[:, h, :].rearrange("p (c i) -> p c i", c=TT),
                                       q32[:, h, :].rearrange("p (c i) -> p c i", c=TT),
                                       repeat(qdec, TT), ALU.mult).then_inc(qd_ready, 1)
                for t in range(TT):
                    wait_apart(pool, v_ready, TT * b + t + 1, pool_passed)
                    for a in range(2):
                        pool.tensor_copy(vm[:, t, a, :].rearrange("p (r a d) -> p r a d", a=2, d=HD)[:, :, a, :],
                                         v[:, t, :].rearrange("p (r a d) -> p r a d", a=2, d=HD)[:, :, a, :]
                                         ).then_inc(vm_ready, 1)

            def core(b, k, par, nxt):
                nxt()
                pool.wait_ge(gs_ready, b + 1)
                n = 0

                def step(ins):
                    nonlocal n
                    n += 1
                    ins.then_inc(gn_ready, 1)
                    wait_apart(pool, gn_ready, 5 * b + n, pool_passed)

                step(pool.tensor_tensor(gn_m[:], gs[:, :, 0], gs[:, :, 0], ALU.mult))
                step(pool.tensor_tensor(gn_m[:], gs[:, :, 1], gn_m[:], ALU.subtract))
                rsqrt_steps(pool, gn_m[:], gn_ve[:], gn_r[:], gn_a[:], gn_chain, RS * b,
                            pool_passed)
                pool.wait_ge(y_ready, 2 * b)
                step(pool.tensor_tensor(gn_s[:], gn_r[:], vec[:, V_GA:V_GA + DH], ALU.mult))
                step(pool.tensor_tensor(gn_m[:], gs[:, :, 0], gn_s[:], ALU.mult))
                step(pool.tensor_tensor(gn_b[:], vec[:, V_BE:V_BE + DH], gn_m[:], ALU.subtract))

            batches(pool, front, core)

        @block.scalar
        def _(act):
            act.wait_ge(consts_in, 16 * 8)
            for i in range(4):
                act.activation((vg_hi[:, :, 0:D] if i == 2 else w_hi[i][:]), wst[:, i], ACT.Copy).then_inc(w_split, 1)
            act.activation(vg_hi[:, :, D:D + E], gst_w[:], ACT.Copy).then_inc(w_split, 1)

            def front(b, k, par, part=None):
                if part in (None, 0):
                    for h in range(DH):
                        act.wait_ge(xnt_ready, 2 * b + h + 1)
                        act.activation(x_hi[:, h, :], fb[h][:], ACT.Copy).then_inc(xhi_ready, 1)
                if part in (None, 1):
                    for j in range(4):
                        h, dst, bias = j % 2, (q32, k32)[j // 2], (V_BQ, V_BK)[j // 2]
                        act.wait_ge(qk_mm, 4 * b + j + 1)
                        act.activation(dst[:, h, :], fb[j % 2][:], ACT.Identity,
                                       bias=vec[:, bias + h:bias + h + 1]).then_inc(qk32, 1)
                        act.wait_ge(qk32, 4 * b + j + 1)
                        if j < 2:
                            act.activation(q_hi[:, h, 0, :], q32[:, h, :], ACT.Copy, scale=parity(0))
                            act.activation(q_hi[:, h, 1, :], q32[:, h, :], ACT.Copy,
                                           scale=parity(1)).then_inc(qk_hi, 1)
                        else:
                            act.activation(k_hi[:, h, :], k32[:, h, :], ACT.Copy).then_inc(qk_hi, 1)
                if part in (None, 2):
                    act.wait_ge(kt_ready, 2 * b + 1)
                    act.activation(kn[:, 0:2, :], fb[0][:].rearrange("p (c d) -> p c d", c=2), ACT.Copy,
                                   scale=kdec).then_inc(kn_ready, 1)
                    act.wait_ge(kt_ready, 2 * b + 2)
                    act.activation(kn[:, 2, :], fb[1][:, 0:D], ACT.Copy, scale=kdec).then_inc(kn_ready, 1)

            def core(b, k, par, nxt):
                act.wait_ge(av_done, 16 * b + 16)
                for h in range(DH):
                    act.activation(a_hi[:, h, :], ob[h][:], ACT.Copy).then_inc(ahi_ready, 1)
                nxt(0)
                for h in range(DH):
                    act.wait_ge(wo_mm, 2 * b + h + 1)
                    act.activation(o32[:, h, :], ob[h][:], ACT.Identity,
                                   bias=vec[:, V_BO + h:V_BO + h + 1]).then_inc(o_ready, 1)
                nxt(1)
                nxt(2)
                act.wait_ge(gn_ready, 5 * b + 5)
                for h in range(DH):
                    act.activation(yT[:, h, :], o32[:, h, :], ACT.Identity, scale=gn_s[:, h:h + 1],
                                   bias=gn_b[:, h:h + 1]).then_inc(y_ready, 1)

            batches(act, front, core)

        @block.vector
        def _(dve):
            dve.wait_ge(consts_in, 16 * 8)
            dve.wait_ge(w_split, 5)
            for i in range(4):
                hi = vg_hi[:, :, 0:D] if i == 2 else w_hi[i][:]
                dve.tensor_tensor(w_lo[i][:], wst[:, i], hi.bitcast(F32), ALU.subtract).then_inc(w_split, 1)
            dve.tensor_tensor(vg_hi[:, :, D + E:], gst_w[:], vg_hi[:, :, D:D + E].bitcast(F32),
                              ALU.subtract).then_inc(w_split, 1)

            def stats(b, k, par):
                dve.wait_ge(x_in[par], 16 * k + 16)
                for t in range(TT):
                    dve.bn_stats(st[:, t, :], xb[par][:, t, :]).then_inc(ln_st, 1)
                wait_apart(dve, ln_st, TT * b + TT, dve_passed)
                for t in range(TT):
                    dve.bn_aggr(mv[:, t, :], st[:, t, :]).then_inc(ln_mv, 1)

            def front(b, k, par, part=None):
                if part in (None, "stats"):
                    stats(b, k, par)
                if part in (None, 0):
                    for h in range(DH):
                        dve.wait_ge(xhi_ready, 2 * b + h + 1)
                        dve.tensor_tensor(x_lo[:, h, :], fb[h][:], x_hi[:, h, :].bitcast(F32),
                                          ALU.subtract).then_inc(xlo_ready, 1)
                if part in (None, 1):
                    for j in range(4):
                        h = j % 2
                        dve.wait_ge(qk_hi, 4 * b + j + 1)
                        if j < 2:
                            for a in range(2):
                                last = dve.scalar_tensor_tensor(q_lo[:, h, a, :], q32[:, h, :], parity(a),
                                                                q_hi[:, h, a, :].bitcast(F32), ALU.mult, ALU.subtract)
                        else:
                            last = dve.tensor_tensor(k_lo[:, h, :], k32[:, h, :], k_hi[:, h, :].bitcast(F32),
                                                     ALU.subtract)
                        last.then_inc(qk_lo, 1)
                if part in (None, 2):
                    dve.wait_ge(vm_ready, 2 * TT * b)
                    for t in range(TT):
                        bank = fb[t % 2]
                        dve.wait_ge(v_mm, TT * b + t + 1)
                        dve.tensor_tensor(v[:, t, :], bank[:, 0:D], bv[:], ALU.add).then_inc(v_ready, 1)
                        dve.tensor_reduce(gsc[:, t, bass.ds(b * E, E)],
                                          bank[:, D:VG].rearrange("p (s e) -> p e s", s=2),
                                          AX.X, ALU.add).then_inc(v_out, 1)

            def core(b, k, par, nxt):
                for n in range(TT * PAIRS):
                    c = n // PAIRS
                    if n % PAIRS == 0 and c < TT - 1:
                        dve.wait_ge(kv_ready, 3 * b + c + 1)
                        dst = state[0] if c == 0 else kvt
                        ins = dve.tensor_tensor(dst[:], cb[c % 2][:, 0:D].rearrange("p (h d) -> p h d", h=DH),
                                                repeat(bdm, DH), ALU.mult)
                        ins.then_inc(kv_read, 1)
                        dve.wait_ge(kv_read, 3 * b + c + 1)
                        if c:
                            dve.scalar_tensor_tensor(state[c][:], state[c - 1][:], DECAY ** P, kvt[:],
                                                     ALU.mult, ALU.add).then_inc(st_ready, 1)
                            dve.wait_ge(st_ready, 2 * b + c)
                    dve.wait_ge(s_mm, 16 * b + n + 1)
                    if n >= 4:
                        dve.wait_ge(av_done, 16 * b + n - 3)
                    dve.tensor_tensor(s_sb[n % 4][:].rearrange("p h a i -> p (h a) i"),
                                      sbk[n % 2][:].rearrange("p (g i) -> p g i", g=4),
                                      repeat(mask, 4), ALU.mult).then_inc(s_ready, 1)
                    if n == 7:
                        nxt("stats")
                for h in range(DH):
                    dve.wait_ge(ahi_ready, 2 * b + h + 1)
                    dve.tensor_tensor(a_lo[:, h, :], ob[h][:], a_hi[:, h, :].bitcast(F32),
                                      ALU.subtract).then_inc(alo_ready, 1)
                nxt(0)
                for h in range(DH):
                    dve.wait_ge(o_ready, 2 * b + h + 1)
                    dve.bn_stats(ost[:, h, :], o32[:, h, :]).then_inc(ost_ready, 1)
                wait_apart(dve, ost_ready, 2 * b + 2, dve_passed)
                for h in range(DH):
                    dve.bn_aggr(gm[:, h, :], ost[:, h, :]).then_inc(omv_ready, 1)
                dve.wait_ge(omv_ready, 2 * b + 2)
                for h in range(DH):
                    dve.scalar_tensor_tensor(gm[:, h, 1:2], gm[:, h, 0:1], gm[:, h, 0:1], gm[:, h, 1:2],
                                             ALU.mult, ALU.add).then_inc(gm_ready, 1)
                nxt(1)
                nxt(2)
                dve.wait_ge(gst_mm, b + 1)
                dve.tensor_copy(gs[:].rearrange("p h s -> p (h s)"), cb[1][:, 0:2 * DH]).then_inc(gs_ready, 1)
                dve.wait_ge(out_stored, 16 * b)
                for j in range(2):
                    dve.wait_ge(yt_mm, 2 * b + j + 1)
                    dve.tensor_tensor(res[:, 2 * j:2 * j + 2, :], ob[j][:].rearrange("p (t c) -> p t c", t=2),
                                      xb[par][:, 2 * j:2 * j + 2, :], ALU.add).then_inc(res_ready, 1)

            batches(dve, front, core)

        @block.tensor
        def _(pe):
            pe.wait_ge(w_split, 10)

            def product(dst, terms):
                for i, (w, m) in enumerate(terms):
                    last = pe.matmul(dst, w, m, start=i == 0, stop=i == len(terms) - 1)
                return last

            def three(hi, lo, mhi, mlo):
                return [(hi, mhi), (hi, mlo), (lo, mhi)]

            def front(b, k, par, part=None):
                if part in (None, 0):
                    pe.wait_ge(xn_ready, TT * b + TT)
                    for h in range(DH):
                        for t in range(TT):
                            last = pe.transpose(fb[h][:, t * P:(t + 1) * P], xn[:, t, h * P:(h + 1) * P], ident)
                        last.then_inc(xnt_ready, 1)
                if part in (None, 1):
                    pe.wait_ge(xlo_ready, 2 * b + 2)
                    for j in range(4):
                        i, h = j // 2, j % 2
                        if j >= 2:
                            pe.wait_ge(qk32, 4 * b + j - 1)
                        cols = slice(h * P, (h + 1) * P)
                        product(fb[j % 2][:], [p for c in range(DH) for p in
                                               three(w_hi[i][:, c, cols], w_lo[i][:, c, cols],
                                                     x_hi[:, c, :], x_lo[:, c, :])]).then_inc(qk_mm, 1)
                if part in (None, 2):
                    for t in range(TT):
                        if t < 2:
                            pe.wait_ge(qk32, 4 * b + t + 3)
                        else:
                            pe.wait_ge(v_out, TT * b + t - 1)
                        toks = slice(t * P, (t + 1) * P)
                        bank = fb[t % 2]
                        n = 0
                        for c in range(DH):
                            pe.matmul(bank[:, 0:VG], x_hi[:, c, toks], vg_hi[:, c, :], start=c == 0, stop=False,
                                      skip_group_check=True)
                            pe.matmul(bank[:, 0:D], x_hi[:, c, toks], w_lo[2][:, c, :], start=False, stop=False,
                                      skip_group_check=True)
                            last = pe.matmul(bank[:, 0:VG], x_lo[:, c, toks], vg_hi[:, c, :], start=False,
                                             stop=c == DH - 1, skip_group_check=True)
                        last.then_inc(v_mm, 1)
                if part in (None, 3):
                    for j in range(2):
                        pe.wait_ge(v_out, TT * b + j + 3)
                        for c in (0, 1) if j == 0 else (2,):
                            for h in range(DH):
                                last = pe.transpose(fb[j][:, (c - 2 * j) * D + h * P:(c - 2 * j) * D + (h + 1) * P],
                                                    k32[:, h, c * P:(c + 1) * P], ident)
                        last.then_inc(kt_ready, 1)

            def scores(b, n):
                c, p = n // PAIRS, n % PAIRS
                if n >= 2:
                    pe.wait_ge(s_ready, 16 * b + n - 1)
                rows = slice(32 * p, 32 * p + 32)
                toks = slice(c * P, (c + 1) * P)
                for h in range(DH):
                    last = product(sbk[n % 2][:, h * 2 * P:(h + 1) * 2 * P],
                                   three(k_hi[rows, h, toks], k_lo[rows, h, toks],
                                         q_hi[rows, h, :, toks], q_lo[rows, h, :, toks]))
                last.then_inc(s_mm, 1)

            def values(b, n):
                c, p = n // PAIRS, n % PAIRS
                toks = slice(c * P, (c + 1) * P)
                if p == 0 and c:
                    if c == 1:
                        pe.wait_ge(kv_read, 3 * b + 1)
                    else:
                        pe.wait_ge(st_ready, 2 * b + c - 1)
                    for h in range(DH):
                        pe.matmul(ob[h][:, toks], state[c - 1][:, h, :], qd[:, h, toks], start=True, stop=False,
                                  skip_group_check=True)
                pe.wait_ge(s_ready, 16 * b + n + 1)
                rows = slice(32 * p, 32 * p + 32)
                for h in range(DH):
                    for a in range(2):
                        last = pe.matmul(ob[h][rows, toks], vm[:, c, a, h * P + 32 * p:h * P + 32 * p + 32],
                                         s_sb[n % 4][:, h, a, :], start=(c == 0 and a == 0), stop=a == 1,
                                         skip_group_check=True)
                last.then_inc(av_done, 1)

            def core(b, k, par, nxt):
                pe.wait_ge(kn_ready, 2 * b + 2)
                pe.wait_ge(vm_ready, 2 * TT * b + 2 * TT)
                pe.wait_ge(qk_lo, 4 * b + 4)
                pe.wait_ge(qd_ready, 2 * b + 2)
                pe.wait_ge(res_ready, 2 * b)
                pe.wait_ge(gs_ready, b)
                for n in range(TT * PAIRS):
                    c = n // PAIRS
                    if n % PAIRS == 0 and c < TT - 1:
                        if c == 2:
                            pe.wait_ge(kv_read, 3 * b + 1)
                        for h in range(DH):
                            last = pe.matmul(cb[c % 2][:, h * P:(h + 1) * P], kn[:, c, h * P:(h + 1) * P],
                                             v[:, c, h * P:(h + 1) * P], start=True, stop=True)
                        last.then_inc(kv_ready, 1)
                    scores(b, n)
                    if n >= 1:
                        values(b, n - 1)
                values(b, TT * PAIRS - 1)
                nxt(0)
                pe.wait_ge(alo_ready, 2 * b + 2)
                for h in range(DH):
                    cols = slice(h * P, (h + 1) * P)
                    product(ob[h][:], [p for c in range(DH) for p in
                                       three(w_hi[3][:, c, cols], w_lo[3][:, c, cols],
                                             a_hi[:, c, :], a_lo[:, c, :])]).then_inc(wo_mm, 1)
                nxt(1)
                nxt(2)
                pe.wait_ge(gm_ready, 2 * b + 2)
                pe.matmul(cb[1][:, 0:2 * DH], gones, gm[:].rearrange("p h s -> p (h s)"),
                          start=True, stop=True).then_inc(gst_mm, 1)
                nxt(3)
                pe.wait_ge(y_ready, 2 * b + 2)
                for j in range(2):
                    for t in range(2):
                        for h in range(DH):
                            last = pe.transpose(ob[j][:, t * D + h * P:t * D + (h + 1) * P],
                                                yT[:, h, (2 * j + t) * P:(2 * j + t + 1) * P], ident)
                    last.then_inc(yt_mm, 1)

            batches(pe, front, core)


def routing_block(nc, cst, gsc, pT, idxT):
    with ExitStack() as ctx:
        def sb(name, shape, dt=F32):
            return ctx.enter_context(nc.sbuf_tensor(name, shape, dt))

        def sem(name):
            return ctx.enter_context(nc.semaphore(name))

        GB = P // E
        W = TT * P
        ROUNDS = CAP // 8
        t0, t1, n_, r_, pw, prob = (sb(n, [P, TT, P]) for n in ("sm_x", "sm_y", "sm_n", "sm_r", "sm_pow", "prob"))
        red = sb("sm_red", [P, TT, GB])
        rows = [sb("rows0", [P, W]), sb("rows1", [P, W])]
        top = sb("top", [P, CAP])
        topi = sb("topi", [P, CAP], U32)
        topf = sb("topf", [P, CAP])
        pst = [ctx.enter_context(nc.psum_tensor(f"route_ps{i}", [P, 512], F32)) for i in range(2)]
        done = sem("route_step")
        prob_ready = sem("prob_ready")
        rows_mm = sem("rows_mm")
        top_ready = sem("top_ready")
        top_mm = sem("top_mm")
        block = ctx.enter_context(nc.Block())
        LOG2E = 1.4426950408889634
        LN2_HI, LN2_LO = 0.693359375, -2.12194440054690581e-4
        ROUND = 12582912.0
        COEF = [1 / 5040, 1 / 720, 1 / 120, 1 / 24, 1 / 6, 0.5, 1.0, 1.0]

        @block.vector
        def _(dve):
            n = 0

            def step(ins):
                nonlocal n
                n += 1
                ins.then_inc(done, 1)
                dve.wait_ge(done, n)

            def by_expert(ap):
                return ap.rearrange("p t (b e) -> p (t b) e", e=E)

            for g in range(2):
                rd = red[:].rearrange("p t b -> p (t b)")
                each = rd.unsqueeze(2).broadcast_to([P, TT * GB, E])
                step(dve.tensor_copy(t0[:], gsc[:, :, g * P:(g + 1) * P]))
                step(dve.tensor_reduce(rd, by_expert(t0[:]), AX.X, ALU.max))
                step(dve.tensor_tensor(by_expert(t1[:]), by_expert(t0[:]), each, ALU.subtract))
                step(dve.tensor_scalar(t1[:], t1[:], -87.0, None, ALU.max))
                step(dve.tensor_scalar(n_[:], t1[:], LOG2E, ROUND, ALU.mult, ALU.add))
                step(dve.tensor_scalar(n_[:], n_[:], ROUND, None, ALU.subtract))
                step(dve.scalar_tensor_tensor(r_[:], n_[:], -LN2_HI, t1[:], ALU.mult, ALU.add))
                step(dve.scalar_tensor_tensor(r_[:], n_[:], -LN2_LO, r_[:], ALU.mult, ALU.add))
                step(dve.tensor_scalar(t0[:], r_[:], COEF[0], COEF[1], ALU.mult, ALU.add))
                for c in COEF[2:]:
                    step(dve.tensor_tensor(t0[:], t0[:], r_[:], ALU.mult))
                    step(dve.tensor_scalar(t0[:], t0[:], c, None, ALU.add))
                step(dve.tensor_scalar(pw[:].bitcast(I32), n_[:], 127.0, float(1 << 23), ALU.add, ALU.mult))
                step(dve.tensor_tensor(t0[:], t0[:], pw[:], ALU.mult))
                step(dve.tensor_reduce(rd, by_expert(t0[:]), AX.X, ALU.add))
                step(dve.reciprocal(rd, rd))
                if g:
                    dve.wait_ge(rows_mm, g)
                dve.tensor_tensor(by_expert(prob[:]), by_expert(t0[:]), each, ALU.mult).then_inc(prob_ready, 1)
                dve.wait_ge(rows_mm, g + 1)
                step(dve.tensor_copy(rows[0][:], pst[0][:]))
                for k in range(ROUNDS):
                    cur, nxt = rows[k % 2], rows[1 - k % 2]
                    col = slice(8 * k, 8 * k + 8)
                    step(dve.max(top[:, col], cur[:]))
                    dve.max_index(topi[:, col], top[:, col], cur[:])
                    step(dve.match_replace(nxt[:], top[:, col], cur[:], -1.0))
                step(dve.tensor_copy(topf[:], topi[:]))
                dve.tensor_scalar(topf[:], topf[:], cst[:, C_OFF + g:C_OFF + g + 1], None,
                                  ALU.add).then_inc(top_ready, 1)
                dve.wait_ge(top_mm, g + 1)
                step(dve.tensor_copy(pT[:, g * P:(g + 1) * P], pst[1][:, 0:P]))
                step(dve.tensor_copy(idxT[:, g * P:(g + 1) * P], pst[1][:, P:2 * P]))

        @block.tensor
        def _(pe):
            ident = cst[:, C_ID:C_ID + P]
            for g in range(2):
                pe.wait_ge(prob_ready, g + 1)
                for t in range(TT):
                    last = pe.transpose(pst[0][:, t * P:(t + 1) * P], prob[:, t, :], ident)
                last.then_inc(rows_mm, 1)
                pe.wait_ge(top_ready, g + 1)
                pe.transpose(pst[1][:, 0:P], top[:], ident)
                pe.transpose(pst[1][:, P:2 * P], topf[:], ident).then_inc(top_mm, 1)


def expert_block(nc, xn_d, out, w1, w2, cst, pT, idxT):
    with ExitStack() as ctx:
        def sb(name, shape, dt=F32):
            return ctx.enter_context(nc.sbuf_tensor(name, shape, dt))

        def ps(name):
            return ctx.enter_context(nc.psum_tensor(name, [P, 512], F32))

        def sem(name):
            return ctx.enter_context(nc.semaphore(name))

        SL = GRP * CAP
        s1 = sb("w1_stage", [P, DH, FF])
        s2 = sb("w2_stage", [P, FT, D])
        w1h, w1l = ([sb(f"w1_{n}{i}", [P, DH, FF], F32R) for i in range(2)] for n in ("hi", "lo"))
        w2h, w2l = ([sb(f"w2_{n}{i}", [P, FT, D], F32R) for i in range(2)] for n in ("hi", "lo"))
        idx = sb("step_idx", [P, GRP], U32)
        sidx = sb("scatter_idx", [P, GRP], U32)
        xg = [sb(f"xg{i}", [P, D]) for i in range(GRP)]
        xt_hi = sb("xt_hi", [P, DH, SL], F32R)
        xt_lo = sb("xt_lo", [P, DH, SL], F32R)
        g32 = [sb(f"g32_{i}", [P, SL]) for i in range(4)]
        g_hi = sb("g_hi", [P, FT, SL], F32R)
        g_lo = sb("g_lo", [P, FT, SL], F32R)
        y = sb("y", [P, GRP, D])
        tb = [ps("xt0"), ps("xt1")]
        hb = [ps(f"hidden{i}") for i in range(4)]
        yb = [ps("y0"), ps("y1")]

        passed = sem("pool_waits_passed")
        w_in = sem("w_in")
        w_hi = sem("w_hi_ready")
        w_lo = sem("w_lo_ready")
        idx_ready = sem("idx_ready")
        sidx_ready = sem("sidx_ready")
        gathered = sem("gathered")
        xt_mm = sem("xt_mm")
        xth = sem("xt_hi_ready")
        xtl = sem("xt_lo_ready")
        h_mm = sem("h_mm")
        g_ready = sem("g_ready")
        gh_ready = sem("g_hi_ready")
        gl_ready = sem("g_lo_ready")
        y_mm = sem("y_mm")
        y_ready = sem("y_ready")
        scattered = sem("scattered")
        PIECES = NG

        w1_v = w1.rearrange("e (h p) f -> e p h f", p=P)
        w2_v = w2.rearrange("e (m p) c -> e p m c", p=P)
        out_rows = out.rearrange("b s c -> (b s) c")
        idx_v = idxT[:].rearrange("p (b e) -> p b e", e=E)
        p_v = pT[:].rearrange("p (b e) -> p b e", e=E)

        def experts(eng, one):
            one(0, 0, True, False)
            one(1, 1, False, False)
            with eng.Fori(1, E // 2 - 1) as i:
                one(2 * i, 0, False, False)
                one(2 * i + 1, 1, False, False)
            one(E - 2, 0, False, False)
            one(E - 1, 1, False, True)

        block = ctx.enter_context(nc.Block())

        @block.sync
        def _(sp):
            def load(e):
                sp.dma_start(s1[:], w1_v[e]).then_inc(w_in, 16)
                sp.dma_start(s2[:], w2_v[e]).then_inc(w_in, 16)

            load(0)

            def one(e, par, first, last):
                if not last:
                    sp.wait_ge(w_lo, PIECES * e + PIECES)
                    load(e + 1)

            experts(sp, one)

        @block.gpsimd
        def _(pool):
            def split(e, par, j):
                h, f = j // (PIECES // DH), j % (PIECES // DH)
                w = FF // (PIECES // DH)
                pieces = ((s1[:, h, f * w:(f + 1) * w], w1h[par][:, h, f * w:(f + 1) * w],
                           w1l[par][:, h, f * w:(f + 1) * w]),
                          (s2[:, j, :], w2h[par][:, j, :], w2l[par][:, j, :]))
                for s, hi, lo in pieces:
                    last = pool.tensor_copy(hi, s)
                last.then_inc(w_hi, 1)
                pool.wait_ge(w_hi, PIECES * e + j + 1)
                for s, hi, lo in pieces:
                    last = pool.tensor_tensor(lo, s, hi.bitcast(F32), ALU.subtract)
                last.then_inc(w_lo, 1)

            def gather(e, g, n):
                wait_apart(pool, gathered, 16 * GRP * n, passed)
                pool.tensor_copy(idx[:].rearrange("p (b o) -> p b o", o=1),
                                 idx_v[:, bass.ds(g * GRP, GRP), bass.ds(e, 1)]).then_inc(idx_ready, 1)
                pool.wait_ge(idx_ready, n + 1)
                wait_apart(pool, xt_mm, 2 * n, passed)
                for k in range(GRP):
                    pool.indirect_dma_start(xg[k][:], None, xn_d,
                                            bass.IndirectOffsetOnAxis(idx[:, k:k + 1], 0)).then_inc(gathered, 16)

            pool.wait_ge(w_in, 32)
            for j in range(PIECES):
                split(0, 0, j)
            gather(0, 0, 0)

            def scatter_now(n):
                pool.wait_ge(scattered, 16 * GRP * n)
                wait_apart(pool, y_ready, GRP * n + GRP, passed)
                for k in range(GRP):
                    pool.indirect_dma_start(out_rows, bass.IndirectOffsetOnAxis(sidx[:, k:k + 1], 0), y[:, k, :],
                                            None, compute_op=ALU.add).then_inc(scattered, 16)

            def take_scatter_indices(e, g, n):
                wait_apart(pool, scattered, 16 * GRP * n, passed)
                pool.tensor_copy(sidx[:].rearrange("p (b o) -> p b o", o=1),
                                 idx_v[:, bass.ds(g * GRP, GRP), bass.ds(e, 1)]).then_inc(sidx_ready, 1)
                pool.wait_ge(sidx_ready, n + 1)

            def one(e, par, first, last):
                def step(g, n):
                    if not last:
                        if isinstance(g, int) and g == 0:
                            wait_apart(pool, w_in, 32 * e + 64, passed)
                    if not (isinstance(g, int) and g == NG - 1):
                        gather(e, g + 1, n + 1)
                    elif not last:
                        gather(e + 1, 0, n + 1)
                    take_scatter_indices(e, g, n)
                    scatter_now(n)

                for g in range(NG):
                    if not last and g == 0:
                        wait_apart(pool, y_mm, GRP * NG * e, passed)
                    step(g, NG * e + g)
                    if not last:
                        split(e + 1, 1 - par, g)

            experts(pool, one)
            pool.wait_ge(scattered, 16 * GRP * NG * E)

        @block.scalar
        def _(act):
            def weighted(e, g, n):
                act.wait_ge(scattered, 16 * GRP * n)
                for k in range(GRP):
                    act.wait_ge(y_mm, GRP * n + k + 1)
                    act.activation(y[:, k, :], yb[k % 2][:, 0:D], ACT.Copy,
                                   scale=p_v[:, bass.ds(g * GRP + k, 1), bass.ds(e, 1)].rearrange("p a o -> p (a o)")
                                   ).then_inc(y_ready, 1)

            def transposed(n):
                for h in range(DH):
                    act.wait_ge(xt_mm, 2 * n + h + 1)
                    act.activation(xt_hi[:, h, :], tb[h][:], ACT.Copy).then_inc(xth, 1)

            def hidden(n):
                for m in range(FT):
                    act.wait_ge(h_mm, FT * n + m + 1)
                    act.wait_ge(gl_ready, FT * n + max(m - 3, 0))
                    act.activation(g32[m % 4][:], hb[m % 4][:], ACT.Gelu).then_inc(g_ready, 1)

            def one(e, par, first, last):
                n0 = NG * e
                transposed(n0)
                if not first:
                    weighted(e - 1, NG - 1, n0 - 1)
                hidden(n0)
                with act.Fori(1, NG) as g:
                    transposed(n0 + g)
                    weighted(e, g - 1, n0 + g - 1)
                    hidden(n0 + g)
                if last:
                    weighted(e, NG - 1, n0 + NG - 1)

            experts(act, one)

        @block.vector
        def _(dve):
            def step(n):
                for h in range(DH):
                    dve.wait_ge(xth, 2 * n + h + 1)
                    dve.tensor_tensor(xt_lo[:, h, :], tb[h][:], xt_hi[:, h, :].bitcast(F32),
                                      ALU.subtract).then_inc(xtl, 1)
                for m in range(FT):
                    dve.wait_ge(g_ready, FT * n + m + 1)
                    dve.tensor_copy(g_hi[:, m, :], g32[m % 4][:]).then_inc(gh_ready, 1)
                    dve.wait_ge(gh_ready, FT * n + m + 1)
                    dve.tensor_tensor(g_lo[:, m, :], g32[m % 4][:], g_hi[:, m, :].bitcast(F32),
                                      ALU.subtract).then_inc(gl_ready, 1)

            with dve.Fori(0, NG * E) as n:
                step(n)

        @block.tensor
        def _(pe):
            ident = cst[:, C_ID:C_ID + P]

            def transposes(n):
                pe.wait_ge(gathered, 16 * GRP * n + 16 * GRP)
                pe.wait_ge(xtl, 2 * n)
                for h in range(DH):
                    for k in range(GRP):
                        last = pe.transpose(tb[h][:, k * P:(k + 1) * P], xg[k][:, h * P:(h + 1) * P], ident)
                    last.then_inc(xt_mm, 1)

            def up(par, n):
                pe.wait_ge(xtl, 2 * n + 2)
                for m in range(FT):
                    if m >= 4:
                        pe.wait_ge(g_ready, FT * n + m - 3)
                    cols = slice(m * P, (m + 1) * P)
                    i = 0
                    for c in range(DH):
                        for w, x_ in ((w1h, xt_hi), (w1h, xt_lo), (w1l, xt_hi)):
                            last = pe.matmul(hb[m % 4][:], w[par][:, c, cols], x_[:, c, :], start=i == 0,
                                             stop=i == 3 * DH - 1)
                            i += 1
                    last.then_inc(h_mm, 1)

            def down(par, n):
                for k in range(GRP):
                    if k == 0:
                        pe.wait_ge(gl_ready, FT * n + FT)
                    pe.wait_ge(y_ready, GRP * n + max(k - 1, 0))
                    cols = slice(k * P, (k + 1) * P)
                    i = 0
                    for m in range(FT):
                        for g_, w in ((g_hi, w2h), (g_hi, w2l), (g_lo, w2h)):
                            last = pe.matmul(yb[k % 2][:, 0:D], g_[:, m, cols], w[par][:, m, :], start=i == 0,
                                             stop=i == 3 * FT - 1)
                            i += 1
                    last.then_inc(y_mm, 1)

            def one(e, par, first, last):
                n0 = NG * e
                transposes(n0)
                if not first:
                    down(1 - par, n0 - 1)
                pe.wait_ge(w_lo, PIECES * e + PIECES)
                up(par, n0)
                with pe.Fori(1, NG) as g:
                    transposes(n0 + g)
                    down(par, n0 + g - 1)
                    up(par, n0 + g)
                if last:
                    down(par, n0 + NG - 1)

            experts(pe, one)


def build(nc, x, wq, wk, wv, wo, gw, w1, w2, bvr, cst_d, vec_d, out):
    xn_d = nc.dram_tensor("xn_rows", [B * S, D], F32).ap()
    with ExitStack() as ctx:
        cst = ctx.enter_context(nc.sbuf_tensor("cst", [P, C_N], F32))
        vec = ctx.enter_context(nc.sbuf_tensor("vec", [P, V_N], F32))
        gsc = ctx.enter_context(nc.sbuf_tensor("gate_scores", [P, TT, BE], F32))
        pT = ctx.enter_context(nc.sbuf_tensor("top_p", [P, BE], F32))
        idxT = ctx.enter_context(nc.sbuf_tensor("top_idx", [P, BE], U32))
        attention_block(nc, x, xn_d, out, wq, wk, wv, wo, gw, bvr, cst_d, vec_d, cst, vec, gsc)
        routing_block(nc, cst, gsc, pT, idxT)
        expert_block(nc, xn_d, out, w1, w2, cst, pT, idxT)


def constants():
    import numpy as np
    i = np.arange(P)
    c = np.zeros((P, C_N), np.float32)
    c[:, C_ID:C_ID + P] = np.eye(P)
    d = (i[None, :] - i[:, None]).astype(np.float32)
    c[:, C_MASK:C_MASK + P] = np.where(d >= 0, np.exp(d * np.log(DECAY)), 0.0)
    same = (i[None, :] // HD) == (i[:, None] // HD)
    c[:, C_G:C_G + P] = same / HD
    c[:, C_BD:C_BD + P] = same
    c[:, C_QD:C_QD + P] = np.exp((i[None, :] + 1.0) * np.log(DECAY))
    for a in range(2):
        c[:, C_PAR + a] = (i // HD) % 2 == a
    c[:, C_KD] = np.exp((P - 1.0 - i) * np.log(DECAY))
    for g in range(2):
        c[:, C_OFF + g] = (g * (P // E) + i // E) * S
    return c


def kernel(L0_attn_x, L0_attn_Wq, L0_attn_bq, L0_attn_Wk, L0_attn_bk, L0_attn_Wv, L0_attn_bv, L0_attn_Wo,
           L0_attn_bo, L0_attn_gamma, L0_attn_beta, L0_ffn_gate_w, L0_ffn_w1, L0_ffn_w2):
    import numpy as np
    import concourse.bacc as bacc
    from concourse.bass_utils import run_bass_kernel_spmd

    def cols(a):
        return np.asarray(a).reshape(DH, P).T

    vec = np.concatenate([cols(a) for a in (L0_attn_bq, L0_attn_bk, L0_attn_bo, L0_attn_gamma, L0_attn_beta)], 1)
    arrays = {
        "x": L0_attn_x, "wq": L0_attn_Wq, "wk": L0_attn_Wk, "wv": L0_attn_Wv, "wo": L0_attn_Wo,
        "gw": L0_ffn_gate_w, "w1": L0_ffn_w1, "w2": L0_ffn_w2,
        "bvr": np.broadcast_to(np.asarray(L0_attn_bv), (P, D)), "cst": constants(), "vec": vec,
    }
    arrays = {f"in_{n}": np.ascontiguousarray(a) for n, a in arrays.items()}
    nc = bacc.Bacc("TRN2", target_bir_lowering=False, num_devices=1)
    args = [nc.dram_tensor(n, list(a.shape), F32, kind="ExternalInput").ap() for n, a in arrays.items()]
    out = nc.dram_tensor("out", [B, S, D], F32, kind="ExternalOutput").ap()
    build(nc, *args, out)
    r = run_bass_kernel_spmd(nc, [arrays], core_ids=[0])
    return r.results[0]["out"]
```

```python
from contextlib import ExitStack

import concourse.bass as bass
from concourse import mybir

F32 = mybir.dt.float32
F32R = mybir.dt.float32r
I32 = mybir.dt.int32
U32 = mybir.dt.uint32
ALU = mybir.AluOpType
ACT = mybir.ActivationFunctionType
AX = mybir.AxisListType

P = 128
B, S, D = 32, 512, 256
HEADS, HD = 16, 16
E, FF = 8, 1024
CAP = 2 * S // E
DH = D // P
TT = S // P
FT = FF // P
PAIRS = P // (2 * HD)
DECAY = 0.95
EPS = 1e-5
MAGIC = 1597463007.0
NEWTON = 3
KV_AT, STATS_AT, NORM_AT, TAIL_AT, TURN_AT = 2, 2, 7, 9, 13
RS = 2 + 4 * NEWTON
GRP = 4
NG = B // GRP
BE = B * E
C_ID, C_MASK, C_G, C_BD, C_QD, C_PAR, C_PPAR, C_KD, C_OFF, C_N = \
    0, 128, 256, 384, 512, 640, 642, 644, 645, 647
V_BQ, V_BK, V_BO, V_GA, V_BE, V_N = 0, 2, 4, 6, 8, 10


def wait_apart(eng, sem, value, passed):
    eng.wait_ge(sem, value)
    if not isinstance(value, int):
        eng.sem_inc(passed, 1)


def rsqrt_steps(eng, var, ve, r, a, chain, base, passed):
    k = 0

    def step(ins):
        nonlocal k
        k += 1
        ins.then_inc(chain, 1)
        wait_apart(eng, chain, base + k, passed)

    step(eng.tensor_scalar(ve, var, EPS, None, ALU.add))
    step(eng.tensor_scalar(r.bitcast(I32), ve.bitcast(I32), -0.5, MAGIC, ALU.mult, ALU.add))
    for _ in range(NEWTON):
        step(eng.tensor_tensor(a, r, r, ALU.mult))
        step(eng.tensor_tensor(a, a, ve, ALU.mult))
        step(eng.tensor_scalar(a, a, -0.5, 1.5, ALU.mult, ALU.add))
        step(eng.tensor_tensor(r, r, a, ALU.mult))


def attention_block(nc, x, xn_d, out, wq, wk, wv, wo, gw, bvr, cst_d, vec_d, cst, vec, gsc):
    with ExitStack() as ctx:
        def sb(name, shape, dt=F32):
            return ctx.enter_context(nc.sbuf_tensor(name, shape, dt))

        def ps(name):
            return ctx.enter_context(nc.psum_tensor(name, [P, 512], F32))

        def sem(name):
            return ctx.enter_context(nc.semaphore(name))

        VG = D + 2 * E
        wst = sb("wst", [P, 4, DH, D])
        gst_w = sb("gate_stage", [P, DH, E])
        bv = sb("bv_rows", [P, D])
        w_hi = [sb(f"w_hi{i}", [P, DH, D], F32R) for i in range(4)]
        w_lo = [sb(f"w_lo{i}", [P, DH, D], F32R) for i in range(4)]
        vg_hi = sb("vg_hi", [P, DH, VG], F32R)
        xb = [sb(f"x{i}", [P, TT, D]) for i in range(2)]
        xn = sb("xn", [P, TT, D])
        st = sb("ln_stats", [P, TT, 6])
        mv = sb("ln_mv", [P, TT, 2])
        ln_ve, ln_r, ln_a = (sb(f"ln_{n}", [P, TT]) for n in ("ve", "r", "a"))
        x_hi = sb("x_hi", [P, DH, S], F32R)
        x_lo = sb("x_lo", [P, DH, S], F32R)
        q32 = sb("q32", [P, DH, S])
        k32 = sb("k32", [P, DH, S])
        q_hi = sb("q_hi", [P, DH, 2, S], F32R)
        q_lo = sb("q_lo", [P, DH, 2, S], F32R)
        k_hi = sb("k_hi", [P, DH, 2, S], F32R)
        k_lo = sb("k_lo", [P, DH, 2, S], F32R)
        qd = sb("q_decayed", [P, DH, S])
        kn = sb("k_natural", [P, TT - 1, D])
        v = sb("v", [P, TT, D])
        vm = sb("v_parity", [P, TT, 2, D])
        s_sb = [sb(f"s_sb{i}", [P, DH, 2, P]) for i in range(4)]
        kvt = sb("kv_masked", [P, DH, P])
        state = [sb(f"state{i}", [P, DH, P]) for i in range(TT - 1)]
        a_hi = sb("a_hi", [P, DH, S], F32R)
        a_lo = sb("a_lo", [P, DH, S], F32R)
        o32 = sb("o32", [P, DH, S])
        ost = sb("o_stats", [P, DH, 6])
        gm = sb("g_moments", [P, DH, 2])
        gs = sb("g_means", [P, DH, 2])
        gn_ve, gn_r, gn_a, gn_m, gn_s, gn_b = (sb(f"gn_{n}", [P, DH]) for n in ("ve", "r", "a", "m", "s", "b"))
        yT = sb("yT", [P, DH, S])
        res = sb("res", [P, TT, D])

        fb = [ps("front0"), ps("front1")]
        sbk = [ps("scores0"), ps("scores1")]
        cb = [ps("misc0"), ps("misc1")]
        ob = [ps("attn0"), ps("attn1")]

        pool_passed = sem("pool_passed")
        dve_passed = sem("dve_passed")
        consts_in = sem("consts_in")
        w_split = sem("w_split")
        vm_zero = sem("vm_zero")
        x_in = [sem("x_in0"), sem("x_in1")]
        ln_st = sem("ln_st")
        ln_mv = sem("ln_mv_ready")
        ln_chain = sem("ln_chain")
        xn_ready = sem("xn_ready")
        xn_stored = sem("xn_stored")
        xnt_ready = sem("xnt_ready")
        xhi_ready = sem("xhi_ready")
        xlo_ready = sem("xlo_ready")
        qk_mm = sem("qk_mm")
        qk32 = sem("qk32_ready")
        qk_hi = sem("qk_hi_ready")
        qk_lo = sem("qk_lo_ready")
        qd_ready = sem("qd_ready")
        v_mm = sem("v_mm")
        v_ready = sem("v_ready")
        v_out = sem("v_bank_read")
        vm_ready = sem("vm_ready")
        kt_ready = sem("kt_ready")
        kn_ready = sem("kn_ready")
        kv_ready = sem("kv_ready")
        kv_read = sem("kv_read")
        st_ready = sem("state_ready")
        s_mm = sem("s_mm")
        s_ready = sem("s_ready")
        av_done = sem("av_done")
        ahi_ready = sem("ahi_ready")
        alo_ready = sem("alo_ready")
        wo_mm = sem("wo_mm")
        o_ready = sem("o_ready")
        ost_ready = sem("ost_ready")
        omv_ready = sem("omv_ready")
        gm_ready = sem("gm_ready")
        gst_mm = sem("gst_mm")
        gs_ready = sem("gs_ready")
        gn_chain = sem("gn_chain")
        gn_ready = sem("gn_ready")
        y_ready = sem("y_ready")
        yt_mm = sem("yt_mm")
        res_in = sem("res_in")
        res_ready = sem("res_ready")
        out_stored = sem("out_stored")

        ident = cst[:, C_ID:C_ID + P]
        mask = cst[:, C_MASK:C_MASK + P]
        gones = cst[:, C_G:C_G + P]
        bdm = cst[:, C_BD:C_BD + P]
        qdec = cst[:, C_QD:C_QD + P]

        def parity(p, of=C_PAR):
            return cst[:, of + p:of + p + 1]

        kdec = cst[:, C_KD:C_KD + 1]

        def repeat(ap, n):
            return ap.unsqueeze(1).broadcast_to([P, n, ap.shape[1]])

        x_v = x.rearrange("b (t p) c -> b p t c", p=P)
        xn_v = xn_d.rearrange("(b t p) c -> b p t c", p=P, t=TT)
        out_v = out.rearrange("b (t p) c -> b p t c", p=P)

        def batches(eng, front, core, tail):
            front(0, 0, 0)
            core(0, 0, 0, lambda part=None: front(1, 0, 1, part), lambda: None)
            core(1, 0, 1, lambda part=None: front(2, 1, 0, part), lambda: tail(0))
            with eng.Fori(1, B // 2 - 1) as i:
                core(2 * i, i, 0, lambda part=None: front(2 * i + 1, i, 1, part), lambda: tail(2 * i - 1))
                core(2 * i + 1, i, 1, lambda part=None: front(2 * i + 2, i + 1, 0, part), lambda: tail(2 * i))
            core(B - 2, B // 2 - 1, 0, lambda part=None: front(B - 1, B // 2 - 1, 1, part), lambda: tail(B - 3))
            core(B - 1, B // 2 - 1, 1, lambda part=None: None, lambda: tail(B - 2))
            tail(B - 1)

        block = ctx.enter_context(nc.Block())

        @block.sync
        def _(sp):
            sp.dma_start(cst[:], cst_d).then_inc(consts_in, 16)
            sp.dma_start(vec[:], vec_d).then_inc(consts_in, 16)
            sp.dma_start(bv[:], bvr).then_inc(consts_in, 16)
            for i, w in enumerate((wq, wk, wv, wo)):
                sp.dma_start(wst[:, i], w.rearrange("(h p) n -> p h n", p=P)).then_inc(consts_in, 16)
            sp.dma_start(gst_w[:], gw.rearrange("(h p) n -> p h n", p=P)).then_inc(consts_in, 16)
            sp.dma_start(xb[0][:], x_v[0]).then_inc(x_in[0], 16)
            sp.dma_start(xb[1][:], x_v[1]).then_inc(x_in[1], 16)

            def front(b, k, par, part=None):
                sp.wait_ge(xn_ready, TT * b + TT)
                sp.dma_start(xn_v[b], xn[:]).then_inc(xn_stored, 16)

            def tail(b):
                sp.wait_ge(res_ready, 2 * b + 2)
                sp.dma_start(out_v[b], res[:]).then_inc(out_stored, 16)

            def core(b, k, par, nxt, prev):
                prev()
                nxt()
                sp.wait_ge(out_stored, 16 * b)
                sp.dma_start(res[:], xb[par][:]).then_inc(res_in, 16)
                if not isinstance(b, int) or b < B - 2:
                    sp.wait_ge(res_in, 16 * b + 16)
                    sp.dma_start(xb[par][:], x_v[b + 2]).then_inc(x_in[par], 16)

            batches(sp, front, core, tail)
            sp.wait_ge(xn_stored, 16 * B)
            sp.wait_ge(out_stored, 16 * B)

        @block.gpsimd
        def _(pool):
            pool.memset(vm[:], 0.0).then_inc(vm_zero, 1)
            pool.wait_ge(consts_in, 16 * 8)
            pool.wait_ge(vm_zero, 1)

            def front(b, k, par, part=None):
                wait_apart(pool, ln_mv, TT * b + TT, pool_passed)
                rsqrt_steps(pool, mv[:, :, 1], ln_ve[:], ln_r[:], ln_a[:], ln_chain, RS * b,
                            pool_passed)
                pool.wait_ge(av_done, 16 * b)
                for h in range(DH):
                    pool.wait_ge(qk32, 4 * b + h + 1)
                    pool.tensor_tensor(qd[:, h, :].rearrange("p (c i) -> p c i", c=TT),
                                       q32[:, h, :].rearrange("p (c i) -> p c i", c=TT),
                                       repeat(qdec, TT), ALU.mult).then_inc(qd_ready, 1)
                for t in range(TT):
                    wait_apart(pool, v_ready, TT * b + t + 1, pool_passed)
                    for a in range(2):
                        pool.tensor_copy(vm[:, t, a, :].rearrange("p (r a d) -> p r a d", a=2, d=HD)[:, :, a, :],
                                         v[:, t, :].rearrange("p (r a d) -> p r a d", a=2, d=HD)[:, :, a, :]
                                         ).then_inc(vm_ready, 1)

            def core(b, k, par, nxt, prev):
                nxt()
                pool.wait_ge(gs_ready, b + 1)
                n = 0

                def step(ins):
                    nonlocal n
                    n += 1
                    ins.then_inc(gn_ready, 1)
                    wait_apart(pool, gn_ready, 5 * b + n, pool_passed)

                step(pool.tensor_tensor(gn_m[:], gs[:, :, 0], gs[:, :, 0], ALU.mult))
                step(pool.tensor_tensor(gn_m[:], gs[:, :, 1], gn_m[:], ALU.subtract))
                rsqrt_steps(pool, gn_m[:], gn_ve[:], gn_r[:], gn_a[:], gn_chain, RS * b,
                            pool_passed)
                pool.wait_ge(y_ready, 2 * b)
                step(pool.tensor_tensor(gn_s[:], gn_r[:], vec[:, V_GA:V_GA + DH], ALU.mult))
                step(pool.tensor_tensor(gn_m[:], gs[:, :, 0], gn_s[:], ALU.mult))
                step(pool.tensor_tensor(gn_b[:], vec[:, V_BE:V_BE + DH], gn_m[:], ALU.subtract))

            batches(pool, front, core, lambda b: None)

        @block.scalar
        def _(act):
            act.wait_ge(consts_in, 16 * 8)
            for i in range(4):
                act.activation((vg_hi[:, :, 0:D] if i == 2 else w_hi[i][:]), wst[:, i], ACT.Copy).then_inc(w_split, 1)
            act.activation(vg_hi[:, :, D:D + E], gst_w[:], ACT.Copy).then_inc(w_split, 1)

            def front(b, k, par, part=None):
                if part in (None, 0):
                    for h in range(DH):
                        act.wait_ge(xnt_ready, 2 * b + h + 1)
                        act.activation(x_hi[:, h, :], fb[h][:], ACT.Copy).then_inc(xhi_ready, 1)
                if part in (None, 1):
                    for j in range(4):
                        h, dst, bias = j % 2, (q32, k32)[j // 2], (V_BQ, V_BK)[j // 2]
                        act.wait_ge(qk_mm, 4 * b + j + 1)
                        act.activation(dst[:, h, :], fb[j % 2][:], ACT.Identity,
                                       bias=vec[:, bias + h:bias + h + 1]).then_inc(qk32, 1)
                        act.wait_ge(qk32, 4 * b + j + 1)
                        src, hi, of = ((q32, q_hi, C_PAR), (k32, k_hi, C_PPAR))[j // 2]
                        act.activation(hi[:, h, 0, :], src[:, h, :], ACT.Copy, scale=parity(0, of))
                        act.activation(hi[:, h, 1, :], src[:, h, :], ACT.Copy,
                                       scale=parity(1, of)).then_inc(qk_hi, 1)
                if part in (None, 2):
                    act.wait_ge(kt_ready, 2 * b + 1)
                    act.activation(kn[:, 0:2, :], fb[0][:].rearrange("p (c d) -> p c d", c=2), ACT.Copy,
                                   scale=kdec).then_inc(kn_ready, 1)
                    act.wait_ge(kt_ready, 2 * b + 2)
                    act.activation(kn[:, 2, :], fb[1][:, 0:D], ACT.Copy, scale=kdec).then_inc(kn_ready, 1)

            def core(b, k, par, nxt, prev):
                nxt(0)
                act.wait_ge(av_done, 16 * b + 16)
                for h in range(DH):
                    act.activation(a_hi[:, h, :], ob[h][:], ACT.Copy).then_inc(ahi_ready, 1)
                nxt(1)
                for h in range(DH):
                    act.wait_ge(wo_mm, 2 * b + h + 1)
                    act.activation(o32[:, h, :], ob[h][:], ACT.Identity,
                                   bias=vec[:, V_BO + h:V_BO + h + 1]).then_inc(o_ready, 1)
                nxt(2)
                act.wait_ge(gn_ready, 5 * b + 5)
                act.wait_ge(yt_mm, 2 * b)
                for h in range(DH):
                    act.activation(yT[:, h, :], o32[:, h, :], ACT.Identity, scale=gn_s[:, h:h + 1],
                                   bias=gn_b[:, h:h + 1]).then_inc(y_ready, 1)

            batches(act, front, core, lambda b: None)

        @block.vector
        def _(dve):
            dve.wait_ge(consts_in, 16 * 8)
            dve.wait_ge(w_split, 5)
            for i in range(4):
                hi = vg_hi[:, :, 0:D] if i == 2 else w_hi[i][:]
                dve.tensor_tensor(w_lo[i][:], wst[:, i], hi.bitcast(F32), ALU.subtract).then_inc(w_split, 1)
            dve.tensor_tensor(vg_hi[:, :, D + E:], gst_w[:], vg_hi[:, :, D:D + E].bitcast(F32),
                              ALU.subtract).then_inc(w_split, 1)

            def stats(b, k, par):
                dve.wait_ge(x_in[par], 16 * k + 16)
                for t in range(TT):
                    dve.bn_stats(st[:, t, :], xb[par][:, t, :]).then_inc(ln_st, 1)
                wait_apart(dve, ln_st, TT * b + TT, dve_passed)
                for t in range(TT):
                    dve.bn_aggr(mv[:, t, :], st[:, t, :]).then_inc(ln_mv, 1)

            def front(b, k, par, part=None):
                if part in (None, "stats"):
                    stats(b, k, par)
                if part in (None, "norm"):
                    wait_apart(dve, ln_chain, RS * b + RS, dve_passed)
                    wait_apart(dve, xn_stored, 16 * b, dve_passed)
                    dve.wait_ge(xnt_ready, 2 * b)
                    for t in range(TT):
                        dve.tensor_scalar(xn[:, t, :], xb[par][:, t, :], mv[:, t, 0:1], ln_r[:, t:t + 1],
                                          ALU.subtract, ALU.mult).then_inc(xn_ready, 1)
                if part in (None, 0):
                    for h in range(DH):
                        dve.wait_ge(xhi_ready, 2 * b + h + 1)
                        dve.tensor_tensor(x_lo[:, h, :], fb[h][:], x_hi[:, h, :].bitcast(F32),
                                          ALU.subtract).then_inc(xlo_ready, 1)
                if part in (None, 1):
                    for j in range(4):
                        h = j % 2
                        dve.wait_ge(qk_hi, 4 * b + j + 1)
                        src, hi, lo, of = ((q32, q_hi, q_lo, C_PAR), (k32, k_hi, k_lo, C_PPAR))[j // 2]
                        for a in range(2):
                            last = dve.scalar_tensor_tensor(lo[:, h, a, :], src[:, h, :], parity(a, of),
                                                            hi[:, h, a, :].bitcast(F32), ALU.mult, ALU.subtract)
                        last.then_inc(qk_lo, 1)
                if part in (None, 2):
                    dve.wait_ge(vm_ready, 2 * TT * b)
                    for t in range(TT):
                        bank = fb[t % 2]
                        dve.wait_ge(v_mm, TT * b + t + 1)
                        dve.tensor_tensor(v[:, t, :], bank[:, 0:D], bv[:], ALU.add).then_inc(v_ready, 1)
                        dve.tensor_reduce(gsc[:, t, bass.ds(b * E, E)],
                                          bank[:, D:VG].rearrange("p (s e) -> p e s", s=2),
                                          AX.X, ALU.add).then_inc(v_out, 1)

            def tail(b):
                dve.wait_ge(res_in, 16 * b + 16)
                for j in range(2):
                    dve.wait_ge(yt_mm, 2 * b + j + 1)
                    r = res[:, 2 * j:2 * j + 2, :]
                    dve.tensor_tensor(r, fb[j][:].rearrange("p (t c) -> p t c", t=2), r,
                                      ALU.add).then_inc(res_ready, 1)

            def core(b, k, par, nxt, prev):
                for n in range(TT * PAIRS):
                    c = n // PAIRS
                    if n % PAIRS == KV_AT and c < TT - 1:
                        dve.wait_ge(kv_ready, 3 * b + c + 1)
                        dst = state[0] if c == 0 else kvt
                        ins = dve.tensor_tensor(dst[:], cb[c % 2][:, 0:D].rearrange("p (h d) -> p h d", h=DH),
                                                repeat(bdm, DH), ALU.mult)
                        ins.then_inc(kv_read, 1)
                        dve.wait_ge(kv_read, 3 * b + c + 1)
                        if c:
                            dve.scalar_tensor_tensor(state[c][:], state[c - 1][:], DECAY ** P, kvt[:],
                                                     ALU.mult, ALU.add).then_inc(st_ready, 1)
                            dve.wait_ge(st_ready, 2 * b + c)
                    dve.wait_ge(s_mm, 16 * b + n + 1)
                    if n >= 4:
                        dve.wait_ge(av_done, 16 * b + n - 3)
                    dve.tensor_tensor(s_sb[n % 4][:].rearrange("p h a i -> p (h a) i"),
                                      sbk[n % 2][:].rearrange("p (g i) -> p g i", g=4),
                                      repeat(mask, 4), ALU.mult).then_inc(s_ready, 1)
                    if n == STATS_AT:
                        nxt("stats")
                    if n == NORM_AT:
                        nxt("norm")
                    if n == TAIL_AT:
                        prev()
                nxt(0)
                for h in range(DH):
                    dve.wait_ge(ahi_ready, 2 * b + h + 1)
                    dve.tensor_tensor(a_lo[:, h, :], ob[h][:], a_hi[:, h, :].bitcast(F32),
                                      ALU.subtract).then_inc(alo_ready, 1)
                nxt(1)
                for h in range(DH):
                    dve.wait_ge(o_ready, 2 * b + h + 1)
                    dve.bn_stats(ost[:, h, :], o32[:, h, :]).then_inc(ost_ready, 1)
                wait_apart(dve, ost_ready, 2 * b + 2, dve_passed)
                for h in range(DH):
                    dve.bn_aggr(gm[:, h, :], ost[:, h, :]).then_inc(omv_ready, 1)
                dve.wait_ge(omv_ready, 2 * b + 2)
                for h in range(DH):
                    dve.scalar_tensor_tensor(gm[:, h, 1:2], gm[:, h, 0:1], gm[:, h, 0:1], gm[:, h, 1:2],
                                             ALU.mult, ALU.add).then_inc(gm_ready, 1)
                nxt(2)
                dve.wait_ge(gst_mm, b + 1)
                dve.tensor_copy(gs[:].rearrange("p h s -> p (h s)"), cb[1][:, 0:2 * DH]).then_inc(gs_ready, 1)
            batches(dve, front, core, tail)

        @block.tensor
        def _(pe):
            pe.wait_ge(w_split, 10)

            def product(dst, terms):
                for i, (w, m) in enumerate(terms):
                    last = pe.matmul(dst, w, m, start=i == 0, stop=i == len(terms) - 1)
                return last

            def three(hi, lo, mhi, mlo):
                return [(hi, mhi), (hi, mlo), (lo, mhi)]

            def front(b, k, par, part=None):
                if part in (None, 0):
                    pe.wait_ge(xn_ready, TT * b + TT)
                    for h in range(DH):
                        for t in range(TT):
                            last = pe.transpose(fb[h][:, t * P:(t + 1) * P], xn[:, t, h * P:(h + 1) * P], ident)
                        last.then_inc(xnt_ready, 1)
                if part in (None, 1):
                    pe.wait_ge(xlo_ready, 2 * b + 2)
                    for j in range(4):
                        i, h = j // 2, j % 2
                        if j >= 2:
                            pe.wait_ge(qk32, 4 * b + j - 1)
                        cols = slice(h * P, (h + 1) * P)
                        product(fb[j % 2][:], [p for c in range(DH) for p in
                                               three(w_hi[i][:, c, cols], w_lo[i][:, c, cols],
                                                     x_hi[:, c, :], x_lo[:, c, :])]).then_inc(qk_mm, 1)
                if part in (None, 2):
                    for t in range(TT):
                        if t < 2:
                            pe.wait_ge(qk32, 4 * b + t + 3)
                        else:
                            pe.wait_ge(v_out, TT * b + t - 1)
                        toks = slice(t * P, (t + 1) * P)
                        bank = fb[t % 2]
                        n = 0
                        for c in range(DH):
                            pe.matmul(bank[:, 0:VG], x_hi[:, c, toks], vg_hi[:, c, :], start=c == 0, stop=False,
                                      skip_group_check=True)
                            pe.matmul(bank[:, 0:D], x_hi[:, c, toks], w_lo[2][:, c, :], start=False, stop=False,
                                      skip_group_check=True)
                            last = pe.matmul(bank[:, 0:VG], x_lo[:, c, toks], vg_hi[:, c, :], start=False,
                                             stop=c == DH - 1, skip_group_check=True)
                        last.then_inc(v_mm, 1)
                if part in (None, 3):
                    for j in range(2):
                        pe.wait_ge(v_out, TT * b + j + 3)
                        for c in (0, 1) if j == 0 else (2,):
                            for h in range(DH):
                                last = pe.transpose(fb[j][:, (c - 2 * j) * D + h * P:(c - 2 * j) * D + (h + 1) * P],
                                                    k32[:, h, c * P:(c + 1) * P], ident)
                        last.then_inc(kt_ready, 1)

            def scores(b, n):
                c, p = n // PAIRS, n % PAIRS
                if n >= 2:
                    pe.wait_ge(s_ready, 16 * b + n - 1)
                rows = slice(64 * (p // 2), 64 * (p // 2) + 64)
                toks = slice(c * P, (c + 1) * P)
                for h in range(DH):
                    last = product(sbk[n % 2][:, h * 2 * P:(h + 1) * 2 * P],
                                   three(k_hi[rows, h, p % 2, toks], k_lo[rows, h, p % 2, toks],
                                         q_hi[rows, h, :, toks], q_lo[rows, h, :, toks]))
                last.then_inc(s_mm, 1)

            def values(b, n):
                c, p = n // PAIRS, n % PAIRS
                toks = slice(c * P, (c + 1) * P)
                if p == 0 and c:
                    if c == 1:
                        pe.wait_ge(kv_read, 3 * b + 1)
                    else:
                        pe.wait_ge(st_ready, 2 * b + c - 1)
                    for h in range(DH):
                        pe.matmul(ob[h][:, toks], state[c - 1][:, h, :], qd[:, h, toks], start=True, stop=False,
                                  skip_group_check=True)
                if p == 0:
                    pe.wait_ge(vm_ready, 2 * TT * b + 2 * c + 2)
                pe.wait_ge(s_ready, 16 * b + n + 1)
                rows = slice(32 * p, 32 * p + 32)
                for h in range(DH):
                    for a in range(2):
                        last = pe.matmul(ob[h][rows, toks], vm[:, c, a, h * P + 32 * p:h * P + 32 * p + 32],
                                         s_sb[n % 4][:, h, a, :], start=(c == 0 and a == 0), stop=a == 1,
                                         skip_group_check=True)
                last.then_inc(av_done, 1)

            def tail(b):
                pe.wait_ge(y_ready, 2 * b + 2)
                for j in range(2):
                    for t in range(2):
                        for h in range(DH):
                            last = pe.transpose(fb[j][:, t * D + h * P:t * D + (h + 1) * P],
                                                yT[:, h, (2 * j + t) * P:(2 * j + t + 1) * P], ident)
                    last.then_inc(yt_mm, 1)

            def core(b, k, par, nxt, prev):
                pe.wait_ge(qk_lo, 4 * b + 4)
                pe.wait_ge(o_ready, 2 * b)
                for n in range(TT * PAIRS):
                    c = n // PAIRS
                    if n % PAIRS == KV_AT and c < TT - 1:
                        if c == 0:
                            pe.wait_ge(kn_ready, 2 * b + 2)
                            pe.wait_ge(qd_ready, 2 * b + 2)
                        if c == 1:
                            pe.wait_ge(gs_ready, b)
                        if c == 2:
                            pe.wait_ge(kv_read, 3 * b + 1)
                        for h in range(DH):
                            last = pe.matmul(cb[c % 2][:, h * P:(h + 1) * P], kn[:, c, h * P:(h + 1) * P],
                                             v[:, c, h * P:(h + 1) * P], start=True, stop=True)
                        last.then_inc(kv_ready, 1)
                    scores(b, n)
                    if n >= 1:
                        values(b, n - 1)
                    if n == TAIL_AT:
                        prev()
                    if n == TURN_AT:
                        pe.wait_ge(res_ready, 2 * b)
                        nxt(0)
                values(b, TT * PAIRS - 1)
                nxt(1)
                pe.wait_ge(alo_ready, 2 * b + 2)
                for h in range(DH):
                    cols = slice(h * P, (h + 1) * P)
                    product(ob[h][:], [p for c in range(DH) for p in
                                       three(w_hi[3][:, c, cols], w_lo[3][:, c, cols],
                                             a_hi[:, c, :], a_lo[:, c, :])]).then_inc(wo_mm, 1)
                nxt(2)
                pe.wait_ge(gm_ready, 2 * b + 2)
                pe.matmul(cb[1][:, 0:2 * DH], gones, gm[:].rearrange("p h s -> p (h s)"),
                          start=True, stop=True).then_inc(gst_mm, 1)
                nxt(3)

            batches(pe, front, core, tail)


def routing_block(nc, cst, gsc, pT, idxT):
    with ExitStack() as ctx:
        def sb(name, shape, dt=F32):
            return ctx.enter_context(nc.sbuf_tensor(name, shape, dt))

        def sem(name):
            return ctx.enter_context(nc.semaphore(name))

        GB = P // E
        W = TT * P
        ROUNDS = CAP // 8
        t0, t1, n_, r_, pw, prob = (sb(n, [P, TT, P]) for n in ("sm_x", "sm_y", "sm_n", "sm_r", "sm_pow", "prob"))
        red = sb("sm_red", [P, TT, GB])
        rows = [sb("rows0", [P, W]), sb("rows1", [P, W])]
        top = sb("top", [P, CAP])
        topi = sb("topi", [P, CAP], U32)
        topf = sb("topf", [P, CAP])
        pst = [ctx.enter_context(nc.psum_tensor(f"route_ps{i}", [P, 512], F32)) for i in range(2)]
        done = sem("route_step")
        prob_ready = sem("prob_ready")
        rows_mm = sem("rows_mm")
        top_ready = sem("top_ready")
        top_mm = sem("top_mm")
        block = ctx.enter_context(nc.Block())
        LOG2E = 1.4426950408889634
        LN2_HI, LN2_LO = 0.693359375, -2.12194440054690581e-4
        ROUND = 12582912.0
        COEF = [1 / 5040, 1 / 720, 1 / 120, 1 / 24, 1 / 6, 0.5, 1.0, 1.0]

        @block.vector
        def _(dve):
            n = 0

            def step(ins):
                nonlocal n
                n += 1
                ins.then_inc(done, 1)
                dve.wait_ge(done, n)

            def by_expert(ap):
                return ap.rearrange("p t (b e) -> p (t b) e", e=E)

            for g in range(2):
                rd = red[:].rearrange("p t b -> p (t b)")
                each = rd.unsqueeze(2).broadcast_to([P, TT * GB, E])
                step(dve.tensor_copy(t0[:], gsc[:, :, g * P:(g + 1) * P]))
                step(dve.tensor_reduce(rd, by_expert(t0[:]), AX.X, ALU.max))
                step(dve.tensor_tensor(by_expert(t1[:]), by_expert(t0[:]), each, ALU.subtract))
                step(dve.tensor_scalar(t1[:], t1[:], -87.0, None, ALU.max))
                step(dve.tensor_scalar(n_[:], t1[:], LOG2E, ROUND, ALU.mult, ALU.add))
                step(dve.tensor_scalar(n_[:], n_[:], ROUND, None, ALU.subtract))
                step(dve.scalar_tensor_tensor(r_[:], n_[:], -LN2_HI, t1[:], ALU.mult, ALU.add))
                step(dve.scalar_tensor_tensor(r_[:], n_[:], -LN2_LO, r_[:], ALU.mult, ALU.add))
                step(dve.tensor_scalar(t0[:], r_[:], COEF[0], COEF[1], ALU.mult, ALU.add))
                for c in COEF[2:]:
                    step(dve.tensor_tensor(t0[:], t0[:], r_[:], ALU.mult))
                    step(dve.tensor_scalar(t0[:], t0[:], c, None, ALU.add))
                step(dve.tensor_scalar(pw[:].bitcast(I32), n_[:], 127.0, float(1 << 23), ALU.add, ALU.mult))
                step(dve.tensor_tensor(t0[:], t0[:], pw[:], ALU.mult))
                step(dve.tensor_reduce(rd, by_expert(t0[:]), AX.X, ALU.add))
                step(dve.reciprocal(rd, rd))
                if g:
                    dve.wait_ge(rows_mm, g)
                dve.tensor_tensor(by_expert(prob[:]), by_expert(t0[:]), each, ALU.mult).then_inc(prob_ready, 1)
                dve.wait_ge(rows_mm, g + 1)
                step(dve.tensor_copy(rows[0][:], pst[0][:]))
                for k in range(ROUNDS):
                    cur, nxt = rows[k % 2], rows[1 - k % 2]
                    col = slice(8 * k, 8 * k + 8)
                    step(dve.max(top[:, col], cur[:]))
                    dve.max_index(topi[:, col], top[:, col], cur[:])
                    step(dve.match_replace(nxt[:], top[:, col], cur[:], -1.0))
                step(dve.tensor_copy(topf[:], topi[:]))
                dve.tensor_scalar(topf[:], topf[:], cst[:, C_OFF + g:C_OFF + g + 1], None,
                                  ALU.add).then_inc(top_ready, 1)
                dve.wait_ge(top_mm, g + 1)
                step(dve.tensor_copy(pT[:, g * P:(g + 1) * P], pst[1][:, 0:P]))
                step(dve.tensor_copy(idxT[:, g * P:(g + 1) * P], pst[1][:, P:2 * P]))

        @block.tensor
        def _(pe):
            ident = cst[:, C_ID:C_ID + P]
            for g in range(2):
                pe.wait_ge(prob_ready, g + 1)
                for t in range(TT):
                    last = pe.transpose(pst[0][:, t * P:(t + 1) * P], prob[:, t, :], ident)
                last.then_inc(rows_mm, 1)
                pe.wait_ge(top_ready, g + 1)
                pe.transpose(pst[1][:, 0:P], top[:], ident)
                pe.transpose(pst[1][:, P:2 * P], topf[:], ident).then_inc(top_mm, 1)


def expert_block(nc, xn_d, out, w1, w2, cst, pT, idxT):
    with ExitStack() as ctx:
        def sb(name, shape, dt=F32):
            return ctx.enter_context(nc.sbuf_tensor(name, shape, dt))

        def ps(name):
            return ctx.enter_context(nc.psum_tensor(name, [P, 512], F32))

        def sem(name):
            return ctx.enter_context(nc.semaphore(name))

        SL = GRP * CAP
        s1 = sb("w1_stage", [P, DH, FF])
        s2 = sb("w2_stage", [P, FT, D])
        w1h, w1l = ([sb(f"w1_{n}{i}", [P, DH, FF], F32R) for i in range(2)] for n in ("hi", "lo"))
        w2h, w2l = ([sb(f"w2_{n}{i}", [P, FT, D], F32R) for i in range(2)] for n in ("hi", "lo"))
        idx = sb("step_idx", [P, GRP], U32)
        sidx = sb("scatter_idx", [P, GRP], U32)
        xg = [sb(f"xg{i}", [P, D]) for i in range(GRP)]
        xt_hi = sb("xt_hi", [P, DH, SL], F32R)
        xt_lo = sb("xt_lo", [P, DH, SL], F32R)
        g32 = [sb(f"g32_{i}", [P, SL]) for i in range(4)]
        g_hi = sb("g_hi", [P, FT, SL], F32R)
        g_lo = sb("g_lo", [P, FT, SL], F32R)
        y = sb("y", [P, GRP, D])
        tb = [ps("xt0"), ps("xt1")]
        hb = [ps(f"hidden{i}") for i in range(4)]
        yb = [ps("y0"), ps("y1")]

        passed = sem("pool_waits_passed")
        w_in = sem("w_in")
        w_hi = sem("w_hi_ready")
        w_lo = sem("w_lo_ready")
        idx_ready = sem("idx_ready")
        sidx_ready = sem("sidx_ready")
        gathered = sem("gathered")
        xt_mm = sem("xt_mm")
        xth = sem("xt_hi_ready")
        xtl = sem("xt_lo_ready")
        h_mm = sem("h_mm")
        g_ready = sem("g_ready")
        gh_ready = sem("g_hi_ready")
        gl_ready = sem("g_lo_ready")
        y_mm = sem("y_mm")
        y_ready = sem("y_ready")
        scattered = sem("scattered")
        PIECES = NG

        w1_v = w1.rearrange("e (h p) f -> e p h f", p=P)
        w2_v = w2.rearrange("e (m p) c -> e p m c", p=P)
        out_rows = out.rearrange("b s c -> (b s) c")
        idx_v = idxT[:].rearrange("p (b e) -> p b e", e=E)
        p_v = pT[:].rearrange("p (b e) -> p b e", e=E)

        def experts(eng, one):
            one(0, 0, True, False)
            one(1, 1, False, False)
            with eng.Fori(1, E // 2 - 1) as i:
                one(2 * i, 0, False, False)
                one(2 * i + 1, 1, False, False)
            one(E - 2, 0, False, False)
            one(E - 1, 1, False, True)

        block = ctx.enter_context(nc.Block())

        @block.sync
        def _(sp):
            def load(e):
                sp.dma_start(s1[:], w1_v[e]).then_inc(w_in, 16)
                sp.dma_start(s2[:], w2_v[e]).then_inc(w_in, 16)

            load(0)

            def one(e, par, first, last):
                if not last:
                    sp.wait_ge(w_lo, PIECES * e + PIECES)
                    load(e + 1)

            experts(sp, one)

        @block.gpsimd
        def _(pool):
            W = DH * FF // PIECES

            def split(e, par, j):
                last = None
                flat = [(s_[:].rearrange("p a f -> p (a f)"), hi[par][:].rearrange("p a f -> p (a f)"),
                         lo[par][:].rearrange("p a f -> p (a f)")) for s_, hi, lo in ((s1, w1h, w1l), (s2, w2h, w2l))]
                for s_, hi, lo in flat:
                    last = pool.tensor_copy(hi[:, bass.ds(j * W, W)], s_[:, bass.ds(j * W, W)])
                last.then_inc(w_hi, 1)
                wait_apart(pool, w_hi, PIECES * e + j + 1, passed)
                for s_, hi, lo in flat:
                    last = pool.tensor_tensor(lo[:, bass.ds(j * W, W)], s_[:, bass.ds(j * W, W)],
                                              hi[:, bass.ds(j * W, W)].bitcast(F32), ALU.subtract)
                last.then_inc(w_lo, 1)

            def take(dst, ready, e, g, n):
                pool.tensor_copy(dst[:].rearrange("p (b o) -> p b o", o=1),
                                 idx_v[:, bass.ds(g * GRP, GRP), bass.ds(e, 1)]).then_inc(ready, 1)
                wait_apart(pool, ready, n + 1, passed)

            def gather(e, g, n):
                wait_apart(pool, gathered, 16 * GRP * n, passed)
                take(idx, idx_ready, e, g, n)
                wait_apart(pool, xt_mm, 2 * n, passed)
                for k in range(GRP):
                    pool.indirect_dma_start(xg[k][:], None, xn_d,
                                            bass.IndirectOffsetOnAxis(idx[:, k:k + 1], 0)).then_inc(gathered, 16)

            def scatter(e, g, n):
                wait_apart(pool, scattered, 16 * GRP * n, passed)
                take(sidx, sidx_ready, e, g, n)
                wait_apart(pool, y_ready, GRP * n + GRP, passed)
                for k in range(GRP):
                    pool.indirect_dma_start(out_rows, bass.IndirectOffsetOnAxis(sidx[:, k:k + 1], 0), y[:, k, :],
                                            None, compute_op=ALU.add).then_inc(scattered, 16)

            pool.wait_ge(w_in, 32)
            for j in range(PIECES):
                split(0, 0, j)
            gather(0, 0, 0)

            def one(e, par, first, last):
                n0 = NG * e
                gather(e, 1, n0 + 1)
                if not first:
                    scatter(e - 1, NG - 1, n0 - 1)
                if not last:
                    wait_apart(pool, w_in, 32 * e + 64, passed)
                    wait_apart(pool, y_mm, GRP * NG * e, passed)
                    split(e + 1, 1 - par, 0)
                with pool.Fori(1, NG - 1) as g:
                    gather(e, g + 1, n0 + g + 1)
                    scatter(e, g - 1, n0 + g - 1)
                    if not last:
                        split(e + 1, 1 - par, g)
                if not last:
                    gather(e + 1, 0, n0 + NG)
                scatter(e, NG - 2, n0 + NG - 2)
                if not last:
                    split(e + 1, 1 - par, NG - 1)

            experts(pool, one)
            scatter(E - 1, NG - 1, NG * E - 1)
            pool.wait_ge(scattered, 16 * GRP * NG * E)

        @block.scalar
        def _(act):
            def weighted(e, g, n):
                act.wait_ge(scattered, 16 * GRP * n)
                for k in range(GRP):
                    act.wait_ge(y_mm, GRP * n + k + 1)
                    act.activation(y[:, k, :], yb[k % 2][:, 0:D], ACT.Copy,
                                   scale=p_v[:, bass.ds(g * GRP + k, 1), bass.ds(e, 1)].rearrange("p a o -> p (a o)")
                                   ).then_inc(y_ready, 1)

            def transposed(n):
                for h in range(DH):
                    act.wait_ge(xt_mm, 2 * n + h + 1)
                    act.activation(xt_hi[:, h, :], tb[h][:], ACT.Copy).then_inc(xth, 1)

            def hidden(n):
                for m in range(FT):
                    act.wait_ge(h_mm, FT * n + m + 1)
                    act.wait_ge(gl_ready, FT * n + max(m - 3, 0))
                    act.activation(g32[m % 4][:], hb[m % 4][:], ACT.Gelu).then_inc(g_ready, 1)

            def one(e, par, first, last):
                n0 = NG * e
                transposed(n0)
                if not first:
                    weighted(e - 1, NG - 1, n0 - 1)
                hidden(n0)
                with act.Fori(1, NG) as g:
                    transposed(n0 + g)
                    weighted(e, g - 1, n0 + g - 1)
                    hidden(n0 + g)
                if last:
                    weighted(e, NG - 1, n0 + NG - 1)

            experts(act, one)

        @block.vector
        def _(dve):
            def step(n):
                for h in range(DH):
                    dve.wait_ge(xth, 2 * n + h + 1)
                    dve.tensor_tensor(xt_lo[:, h, :], tb[h][:], xt_hi[:, h, :].bitcast(F32),
                                      ALU.subtract).then_inc(xtl, 1)
                for m in range(FT):
                    dve.wait_ge(g_ready, FT * n + m + 1)
                    dve.tensor_copy(g_hi[:, m, :], g32[m % 4][:]).then_inc(gh_ready, 1)
                    dve.wait_ge(gh_ready, FT * n + m + 1)
                    dve.tensor_tensor(g_lo[:, m, :], g32[m % 4][:], g_hi[:, m, :].bitcast(F32),
                                      ALU.subtract).then_inc(gl_ready, 1)

            with dve.Fori(0, NG * E) as n:
                step(n)

        @block.tensor
        def _(pe):
            ident = cst[:, C_ID:C_ID + P]

            def transposes(n):
                pe.wait_ge(gathered, 16 * GRP * n + 16 * GRP)
                pe.wait_ge(xtl, 2 * n)
                for h in range(DH):
                    for k in range(GRP):
                        last = pe.transpose(tb[h][:, k * P:(k + 1) * P], xg[k][:, h * P:(h + 1) * P], ident)
                    last.then_inc(xt_mm, 1)

            def up(par, n):
                pe.wait_ge(xtl, 2 * n + 2)
                for m in range(FT):
                    if m >= 4:
                        pe.wait_ge(g_ready, FT * n + m - 3)
                    cols = slice(m * P, (m + 1) * P)
                    i = 0
                    for c in range(DH):
                        for w, x_ in ((w1h, xt_hi), (w1h, xt_lo), (w1l, xt_hi)):
                            last = pe.matmul(hb[m % 4][:], w[par][:, c, cols], x_[:, c, :], start=i == 0,
                                             stop=i == 3 * DH - 1)
                            i += 1
                    last.then_inc(h_mm, 1)

            def down(par, n):
                for k in range(GRP):
                    if k == 0:
                        pe.wait_ge(gl_ready, FT * n + FT)
                    pe.wait_ge(y_ready, GRP * n + max(k - 1, 0))
                    cols = slice(k * P, (k + 1) * P)
                    i = 0
                    for m in range(FT):
                        for g_, w in ((g_hi, w2h), (g_hi, w2l), (g_lo, w2h)):
                            last = pe.matmul(yb[k % 2][:, 0:D], g_[:, m, cols], w[par][:, m, :], start=i == 0,
                                             stop=i == 3 * FT - 1)
                            i += 1
                    last.then_inc(y_mm, 1)

            def one(e, par, first, last):
                n0 = NG * e
                transposes(n0)
                if not first:
                    down(1 - par, n0 - 1)
                pe.wait_ge(w_lo, PIECES * e + PIECES)
                up(par, n0)
                with pe.Fori(1, NG) as g:
                    transposes(n0 + g)
                    down(par, n0 + g - 1)
                    up(par, n0 + g)
                if last:
                    down(par, n0 + NG - 1)

            experts(pe, one)


def build(nc, x, wq, wk, wv, wo, gw, w1, w2, bvr, cst_d, vec_d, out):
    xn_d = nc.dram_tensor("xn_rows", [B * S, D], F32).ap()
    with ExitStack() as ctx:
        cst = ctx.enter_context(nc.sbuf_tensor("cst", [P, C_N], F32))
        vec = ctx.enter_context(nc.sbuf_tensor("vec", [P, V_N], F32))
        gsc = ctx.enter_context(nc.sbuf_tensor("gate_scores", [P, TT, BE], F32))
        pT = ctx.enter_context(nc.sbuf_tensor("top_p", [P, BE], F32))
        idxT = ctx.enter_context(nc.sbuf_tensor("top_idx", [P, BE], U32))
        attention_block(nc, x, xn_d, out, wq, wk, wv, wo, gw, bvr, cst_d, vec_d, cst, vec, gsc)
        routing_block(nc, cst, gsc, pT, idxT)
        expert_block(nc, xn_d, out, w1, w2, cst, pT, idxT)


def constants():
    import numpy as np
    i = np.arange(P)
    c = np.zeros((P, C_N), np.float32)
    c[:, C_ID:C_ID + P] = np.eye(P)
    d = (i[None, :] - i[:, None]).astype(np.float32)
    c[:, C_MASK:C_MASK + P] = np.where(d >= 0, np.exp(d * np.log(DECAY)), 0.0)
    same = (i[None, :] // HD) == (i[:, None] // HD)
    c[:, C_G:C_G + P] = same / HD
    c[:, C_BD:C_BD + P] = same
    c[:, C_QD:C_QD + P] = np.exp((i[None, :] + 1.0) * np.log(DECAY))
    for a in range(2):
        c[:, C_PAR + a] = (i // HD) % 2 == a
        c[:, C_PPAR + a] = (i // (2 * HD)) % 2 == a
    c[:, C_KD] = np.exp((P - 1.0 - i) * np.log(DECAY))
    for g in range(2):
        c[:, C_OFF + g] = (g * (P // E) + i // E) * S
    return c


def kernel(L0_attn_x, L0_attn_Wq, L0_attn_bq, L0_attn_Wk, L0_attn_bk, L0_attn_Wv, L0_attn_bv, L0_attn_Wo,
           L0_attn_bo, L0_attn_gamma, L0_attn_beta, L0_ffn_gate_w, L0_ffn_w1, L0_ffn_w2):
    import numpy as np
    import concourse.bacc as bacc
    from concourse.bass_utils import run_bass_kernel_spmd

    def cols(a):
        return np.asarray(a).reshape(DH, P).T

    vec = np.concatenate([cols(a) for a in (L0_attn_bq, L0_attn_bk, L0_attn_bo, L0_attn_gamma, L0_attn_beta)], 1)
    arrays = {
        "x": L0_attn_x, "wq": L0_attn_Wq, "wk": L0_attn_Wk, "wv": L0_attn_Wv, "wo": L0_attn_Wo,
        "gw": L0_ffn_gate_w, "w1": L0_ffn_w1, "w2": L0_ffn_w2,
        "bvr": np.broadcast_to(np.asarray(L0_attn_bv), (P, D)), "cst": constants(), "vec": vec,
    }
    arrays = {f"in_{n}": np.ascontiguousarray(a) for n, a in arrays.items()}
    nc = bacc.Bacc("TRN2", target_bir_lowering=False, num_devices=1)
    args = [nc.dram_tensor(n, list(a.shape), F32, kind="ExternalInput").ap() for n, a in arrays.items()]
    out = nc.dram_tensor("out", [B, S, D], F32, kind="ExternalOutput").ap()
    build(nc, *args, out)
    r = run_bass_kernel_spmd(nc, [arrays], core_ids=[0])
    return r.results[0]["out"]
```

```python
from contextlib import ExitStack

import concourse.bass as bass
from concourse import mybir

F32 = mybir.dt.float32
F32R = mybir.dt.float32r
I32 = mybir.dt.int32
U32 = mybir.dt.uint32
ALU = mybir.AluOpType
ACT = mybir.ActivationFunctionType
AX = mybir.AxisListType

P = 128
B, S, D = 32, 512, 256
HEADS, HD = 16, 16
E, FF = 8, 1024
CAP = 2 * S // E
DH = D // P
TT = S // P
FT = FF // P
PAIRS = P // (2 * HD)
DECAY = 0.95
EPS = 1e-5
MAGIC = 1597463007.0
NEWTON = 3
JOBS = TT * PAIRS
SUM_AT = (1, 2, 10)
STATE_AT = (2, 3, 10)
STATS_AT = 3
MOMENTS_AT, MEANS_AT = 4, 5
ROUND_AT = 11
SOFTMAX_ODD, SOFTMAX_EVEN = (7, 8, 9, 10, 10, 11, 11, 12, 12, 13, 13, 14, 14, 15, 15), (4, 5, 6, 7)
ROWS_AT = 9
RS = 2 + 4 * NEWTON
LS = RS + 2
GRP = 4
NG = B // GRP
BE = B * E
C_ID, C_MASK, C_G, C_BD, C_QD, C_PAR, C_PPAR, C_KD, C_OFF, C_N = \
    0, 128, 256, 384, 512, 640, 642, 644, 645, 647
V_BQ, V_BK, V_BO, V_GA, V_BE, V_N = 0, 2, 4, 6, 8, 10


def wait_apart(eng, sem, value, passed):
    eng.wait_ge(sem, value)
    if not isinstance(value, int):
        eng.sem_inc(passed, 1)


def rsqrt_steps(eng, var, ve, r, a, chain, base, passed):
    k = 0

    def step(ins):
        nonlocal k
        k += 1
        ins.then_inc(chain, 1)
        wait_apart(eng, chain, base + k, passed)

    step(eng.tensor_scalar(ve, var, EPS, None, ALU.add))
    step(eng.tensor_scalar(r.bitcast(I32), ve.bitcast(I32), -0.5, MAGIC, ALU.mult, ALU.add))
    for _ in range(NEWTON):
        step(eng.tensor_tensor(a, r, r, ALU.mult))
        step(eng.tensor_tensor(a, a, ve, ALU.mult))
        step(eng.tensor_scalar(a, a, -0.5, 1.5, ALU.mult, ALU.add))
        step(eng.tensor_tensor(r, r, a, ALU.mult))


class Routing:
    GB = P // E
    ROUNDS = CAP // 8
    LOG2E = 1.4426950408889634
    LN2_HI, LN2_LO = 0.693359375, -2.12194440054690581e-4
    ROUND = 12582912.0
    COEF = [1 / 5040, 1 / 720, 1 / 120, 1 / 24, 1 / 6, 0.5, 1.0, 1.0]
    STEPS = 19
    LAST_PASS_ROUNDS = 4
    STEP_ROUNDS = 4
    LAST_STEP = (ROUNDS - LAST_PASS_ROUNDS) // STEP_ROUNDS

    def __init__(self, ctx, nc, cst):
        def sb(name, shape, dt=F32):
            return ctx.enter_context(nc.sbuf_tensor(name, shape, dt))

        def sem(name):
            return ctx.enter_context(nc.semaphore(name))

        self.cst = cst
        self.score = sb("gate_scores", [P, TT, BE])
        self.t, self.q, self.n, self.r, self.pw = (sb(f"softmax_{n}", [P, TT, 2 * E]) for n in "tqnrw")
        self.red = sb("softmax_red", [P, TT, 2])
        self.rows = [sb("rows0", [P, S]), sb("rows1", [P, S])]
        self.best = sb("best", [P, 8])
        self.besti = sb("best_index", [P, 8], U32)
        self.top = sb("top", [P, CAP])
        self.topi = sb("topi", [P, CAP], U32)
        self.topf = self.rows[1][:, 0:CAP]
        self.pT = sb("top_p", [P, BE])
        self.idxT = sb("top_idx", [P, BE], U32)
        self.soft = sem("softmax_step")
        self.rows_mm = sem("rows_mm")
        self.rows_ready = sem("rows_ready")
        self.max_ready = sem("max_ready")
        self.index_ready = sem("index_ready")
        self.replaced = sem("replaced")
        self.kept = sem("kept")
        self.top_float = sem("top_float")
        self.top_ready = sem("top_ready")
        self.top_mm = sem("top_mm")
        self.chosen = sem("chosen")

    def softmax_step(self, dve, pair, k, scored):
        def experts(ap):
            return ap.rearrange("p t (b e) -> p t b e", e=E)

        g = experts(self.score[:, :, bass.ds(pair * 2 * E, 2 * E)])
        t, q, n, r, pw = (experts(a[:]) for a in (self.t, self.q, self.n, self.r, self.pw))
        red = self.red[:]
        each = red.unsqueeze(3).broadcast_to([P, TT, 2, E])
        if k == 0:
            wait_apart(dve, scored, 2 * TT * pair + 2 * TT, self.passed)
        else:
            dve.wait_ge(self.soft, self.STEPS * pair + k)
        if k == 0:
            ins = dve.tensor_reduce(red, g, AX.X, ALU.max)
        elif k == 1:
            ins = dve.tensor_tensor(t, g, each, ALU.subtract)
        elif k == 2:
            ins = dve.tensor_scalar(t, t, -87.0, None, ALU.max)
        elif k == 3:
            ins = dve.tensor_scalar(n, t, self.LOG2E, self.ROUND, ALU.mult, ALU.add)
        elif k == 4:
            ins = dve.tensor_scalar(n, n, self.ROUND, None, ALU.subtract)
        elif k == 5:
            ins = dve.scalar_tensor_tensor(r, n, -self.LN2_HI, t, ALU.mult, ALU.add)
        elif k == 6:
            ins = dve.scalar_tensor_tensor(r, n, -self.LN2_LO, r, ALU.mult, ALU.add)
        elif k == 7:
            ins = dve.tensor_scalar(q, r, self.COEF[0], None, ALU.mult)
        elif k < 14:
            ins = dve.scalar_tensor_tensor(q, q, self.COEF[k - 7], r, ALU.add, ALU.mult)
        elif k == 14:
            ins = dve.tensor_scalar(pw.bitcast(I32), n, 127.0, float(1 << 23), ALU.add, ALU.mult)
        elif k == 15:
            ins = dve.scalar_tensor_tensor(q, q, self.COEF[7], pw, ALU.add, ALU.mult)
        elif k == 16:
            ins = dve.tensor_reduce(red, q, AX.X, ALU.add)
        elif k == 17:
            ins = dve.reciprocal(red, red)
        elif k == 18:
            ins = dve.tensor_tensor(g, q, each, ALU.mult)
        ins.then_inc(self.soft, 1)

    def turn_rows(self, pe, g, bank):
        pe.wait_ge(self.soft, self.STEPS * self.GB // 2 * (g + 1))
        for t in range(TT):
            last = pe.transpose(bank[:, t * P:(t + 1) * P], self.score[:, t, g * P:(g + 1) * P],
                                self.cst[:, C_ID:C_ID + P])
        last.then_inc(self.rows_mm, 1)

    def take_rows(self, dve, g, bank):
        dve.wait_ge(self.rows_mm, g + 1)
        dve.tensor_copy(self.rows[0][:], bank[:]).then_inc(self.rows_ready, 1)

    def top_eight(self, dve, g, k, par):
        wait_apart(dve, self.rows_ready, g + 1, self.passed)
        wait_apart(dve, self.replaced, self.ROUNDS * g + k, self.passed)
        wait_apart(dve, self.kept, 2 * (self.ROUNDS * g + k), self.passed)
        dve.max(self.best[:], self.rows[par][:]).then_inc(self.max_ready, 1)

    def their_index(self, dve, g, k, par):
        wait_apart(dve, self.max_ready, self.ROUNDS * g + k + 1, self.passed)
        dve.max_index(self.besti[:], self.best[:], self.rows[par][:]).then_inc(self.index_ready, 1)

    def strike(self, dve, g, k, par):
        dve.match_replace(self.rows[1 - par][:], self.best[:], self.rows[par][:],
                          -1.0).then_inc(self.replaced, 1)
        col = bass.ds(8 * k, 8)
        if g:
            dve.wait_ge(self.top_mm, g)
        dve.tensor_copy(self.top[:, col], self.best[:]).then_inc(self.kept, 1)
        wait_apart(dve, self.index_ready, self.ROUNDS * g + k + 1, self.passed)
        dve.tensor_copy(self.topi[:, col], self.besti[:]).then_inc(self.kept, 1)

    def whole_round(self, dve, g, k):
        self.top_eight(dve, g, k, k % 2)
        self.their_index(dve, g, k, k % 2)
        self.strike(dve, g, k, k % 2)

    def as_float(self, dve, g):
        dve.wait_ge(self.kept, 2 * self.ROUNDS * (g + 1))
        dve.tensor_copy(self.topf, self.topi[:]).then_inc(self.top_float, 1)
        dve.wait_ge(self.top_float, g + 1)
        dve.tensor_scalar(self.topf, self.topf, self.cst[:, C_OFF + g:C_OFF + g + 1], None,
                          ALU.add).then_inc(self.top_ready, 1)

    def turn_top(self, pe, g, bank):
        pe.wait_ge(self.top_ready, g + 1)
        ident = self.cst[:, C_ID:C_ID + P]
        pe.transpose(bank[:, 0:P], self.top[:], ident)
        pe.transpose(bank[:, P:2 * P], self.topf, ident).then_inc(self.top_mm, 1)

    def take_top(self, dve, g, bank):
        dve.wait_ge(self.top_mm, g + 1)
        dve.tensor_copy(self.pT[:, g * P:(g + 1) * P], bank[:, 0:P]).then_inc(self.chosen, 1)
        dve.tensor_copy(self.idxT[:, g * P:(g + 1) * P], bank[:, P:2 * P]).then_inc(self.chosen, 1)


def attention_block(nc, x, xn_d, out, wq, wk, wv, wo, gw, w1, bvr, cst_d, vec_d, cst, vec,
                    route, s1, w_in, res, out_stored):
    with ExitStack() as ctx:
        def sb(name, shape, dt=F32):
            return ctx.enter_context(nc.sbuf_tensor(name, shape, dt))

        def ps(name):
            return ctx.enter_context(nc.psum_tensor(name, [P, 512], F32))

        def sem(name):
            return ctx.enter_context(nc.semaphore(name))

        VG = D + 2 * E
        wst = s1[:].rearrange("p h (i n) -> p (h i) n", n=D).rearrange("p (i h) n -> p i h n", h=DH)
        gst_w = sb("gate_stage", [P, DH, E])
        bv = sb("bv_rows", [P, D])
        w_hi = [None if i == 2 else sb(f"w_hi{i}", [P, DH, D], F32R) for i in range(4)]
        w_lo = [sb(f"w_lo{i}", [P, DH, D], F32R) for i in range(4)]
        vg_hi = sb("vg_hi", [P, DH, VG], F32R)
        xb = [sb(f"x{i}", [P, TT, D]) for i in range(2)]
        xn = sb("xn", [P, TT, D])
        vraw = sb("v_unbiased", [P, 2, VG])
        st = sb("ln_stats", [P, TT, 6])
        mv = sb("ln_mv", [P, TT, 2])
        ln_ve, ln_r, ln_a, ln_m = (sb(f"ln_{n}", [P, TT]) for n in ("ve", "r", "a", "m"))
        x_hi = sb("x_hi", [P, DH, S], F32R)
        x_lo = sb("x_lo", [P, DH, S], F32R)
        q32 = sb("q32", [P, DH, S])
        k32 = sb("k32", [P, DH, S])
        q_hi = [sb(f"q_hi{i}", [P, DH, 2, S], F32R) for i in range(2)]
        q_lo = [sb(f"q_lo{i}", [P, DH, 2, S], F32R) for i in range(2)]
        k_hi = [sb(f"k_hi{i}", [P, DH, 2, S], F32R) for i in range(2)]
        k_lo = [sb(f"k_lo{i}", [P, DH, 2, S], F32R) for i in range(2)]
        qd = [sb(f"q_decayed{i}", [P, DH, S]) for i in range(2)]
        kn = [sb(f"k_natural{i}", [P, TT - 1, D]) for i in range(2)]
        v = [sb(f"v{i}", [P, TT, D]) for i in range(2)]
        vm = [sb(f"v_parity{i}", [P, TT, 2, D]) for i in range(2)]
        s_sb = [sb(f"s_sb{i}", [P, DH, 2, P]) for i in range(2 * PAIRS)]
        state = [sb(f"state{i}", [P, DH, P]) for i in range(TT - 1)]
        a_hi = sb("a_hi", [P, DH, S], F32R)
        a_lo = sb("a_lo", [P, DH, S], F32R)
        o32 = sb("o32", [P, DH, S])
        ost = sb("o_stats", [P, DH, 6])
        gm = sb("g_moments", [P, DH, 2])
        gs = sb("g_means", [P, DH, 2])
        gn_ve, gn_r, gn_a, gn_m, gn_s, gn_b = (sb(f"gn_{n}", [P, DH]) for n in ("ve", "r", "a", "m", "s", "b"))

        fb = [ps("front0"), ps("front1")]
        sbk = [ps("scores0"), ps("scores1")]
        cb = [ps("misc0"), ps("misc1")]
        ob = [ps("attn0"), ps("attn1")]

        pool_passed = sem("pool_passed")
        dve_passed = sem("dve_passed")
        route.passed = dve_passed
        consts_in = sem("consts_in")
        w_hi_act = sem("w_hi_by_act")
        w_hi_pool = sem("w_hi_by_pool")
        w_split = sem("w_split")
        vm_zero = sem("vm_zero")
        x_in = [sem("x_in0"), sem("x_in1")]
        ln_st = sem("ln_st")
        ln_mv = sem("ln_mv_ready")
        ln_chain = sem("ln_chain")
        xn_ready = sem("xn_ready")
        xn_stored = sem("xn_stored")
        xnt_ready = sem("xnt_ready")
        xhi_ready = sem("xhi_ready")
        xlo_ready = sem("xlo_ready")
        qk_mm = sem("qk_mm")
        qk32 = sem("qk32_ready")
        qk_hi = sem("qk_hi_ready")
        qk_lo = sem("qk_lo_ready")
        qd_ready = sem("qd_ready")
        v_mm = sem("v_mm")
        v_ready = sem("v_ready")
        v_out = sem("v_bank_read")
        vm_ready = sem("vm_ready")
        scored = sem("scored")
        kt_ready = sem("kt_ready")
        kn_ready = sem("kn_ready")
        kv_ready = sem("kv_ready")
        kv_read = sem("kv_read")
        st_ready = sem("state_ready")
        s_mm = sem("s_mm")
        s_ready = sem("s_ready")
        av_done = sem("av_done")
        ahi_ready = sem("ahi_ready")
        alo_ready = sem("alo_ready")
        wo_mm = sem("wo_mm")
        o_ready = sem("o_ready")
        ost_ready = sem("ost_ready")
        omv_ready = sem("omv_ready")
        gm_ready = sem("gm_ready")
        gst_mm = sem("gst_mm")
        gs_ready = sem("gs_ready")
        gn_chain = sem("gn_chain")
        gn_ready = sem("gn_ready")
        y_ready = sem("y_ready")
        yt_mm = sem("yt_mm")
        res_in = sem("res_in")
        res_ready = sem("res_ready")

        ident = cst[:, C_ID:C_ID + P]
        mask = cst[:, C_MASK:C_MASK + P]
        gones = cst[:, C_G:C_G + P]
        bdm = cst[:, C_BD:C_BD + P]
        qdec = cst[:, C_QD:C_QD + P]

        def parity(p, of=C_PAR):
            return cst[:, of + p:of + p + 1]

        kdec = cst[:, C_KD:C_KD + 1]

        def repeat(ap, n):
            return ap.unsqueeze(1).broadcast_to([P, n, ap.shape[1]])

        x_v = x.rearrange("b (t p) c -> b p t c", p=P)
        xn_v = xn_d.rearrange("(b t p) c -> b p t c", p=P, t=TT)
        out_v = out.rearrange("b (t p) c -> b p t c", p=P)

        def passes(eng, one):
            MID = Routing.GB
            one(-1, 1)
            one(0, 0)
            one(1, 1)
            with eng.Fori(1, MID // 2) as i:
                one(2 * i, 0)
                one(2 * i + 1, 1)
            one(MID, 0)
            one(MID + 1, 1)
            with eng.Fori(MID // 2 + 1, B // 2 - 2) as i:
                one(2 * i, 0)
                one(2 * i + 1, 1)
            for b in range(B - 4, B + 1):
                one(b, b % 2)

        def has(b):
            return not isinstance(b, int) or 0 <= b < B

        def least(value):
            return max(value, 0) if isinstance(value, int) else value

        block = ctx.enter_context(nc.Block())

        @block.sync
        def _(sp):
            sp.dma_start(xb[0][:], x_v[0]).then_inc(x_in[0], 16)
            sp.dma_start(cst[:], cst_d).then_inc(consts_in, 16)
            sp.dma_start(vec[:], vec_d).then_inc(consts_in, 16)
            sp.dma_start(bv[:], bvr).then_inc(consts_in, 16)
            for i, w in enumerate((wq, wk, wv, wo)):
                sp.dma_start(wst[:, i], w.rearrange("(h p) n -> p h n", p=P)).then_inc(consts_in, 16)
            sp.dma_start(gst_w[:], gw.rearrange("(h p) n -> p h n", p=P)).then_inc(consts_in, 16)
            sp.dma_start(xb[1][:], x_v[1]).then_inc(x_in[1], 16)
            sp.wait_ge(w_split, 5)
            sp.dma_start(s1[:], w1[0].rearrange("(h p) f -> p h f", p=P)).then_inc(w_in, 16)

            def normed(l, par):
                sp.wait_ge(xn_ready, TT * l + TT)
                sp.dma_start(xn_v[l], xn[:]).then_inc(xn_stored, 16)
                if has(l + 2):
                    sp.dma_start(xb[par][:], x_v[l + 2]).then_inc(x_in[par], 16)

            normed(0, 0)

            def one(b, par):
                if has(b - 2):
                    sp.wait_ge(res_ready, 2 * b - 2)
                    sp.dma_start(out_v[b - 2], res[:]).then_inc(out_stored, 16)
                if has(b - 1):
                    sp.wait_ge(out_stored, least(16 * b - 16))
                    sp.dma_start(res[:], x_v[b - 1]).then_inc(res_in, 16)
                if has(b + 2):
                    normed(b + 2, par)

            passes(sp, one)
            sp.wait_ge(res_ready, 2 * B)
            sp.dma_start(out_v[B - 1], res[:]).then_inc(out_stored, 16)
            sp.wait_ge(xn_stored, 16 * B)

        @block.gpsimd
        def _(pool):
            for i in range(2):
                pool.memset(vm[i][:], 0.0).then_inc(vm_zero, 1)

            def ln_factor(l):
                wait_apart(pool, ln_mv, TT * l + TT, pool_passed)
                pool.tensor_scalar(ln_m[:], mv[:, :, 0], -1.0, None, ALU.mult).then_inc(ln_chain, 1)
                rsqrt_steps(pool, mv[:, :, 1], ln_ve[:], ln_r[:], ln_a[:], ln_chain, LS * l + 1,
                            pool_passed)
                pool.tensor_tensor(ln_m[:], ln_m[:], ln_r[:], ALU.mult).then_inc(ln_chain, 1)

            ln_factor(0)
            pool.wait_ge(consts_in, 16 * 8)
            pool.tensor_copy(w_hi[3][:], wst[:, 3]).then_inc(w_hi_pool, 1)
            pool.tensor_copy(vg_hi[:, :, D:D + E], gst_w[:]).then_inc(w_hi_pool, 1)
            pool.wait_ge(vm_zero, 2)

            def one(b, par):
                f, fp, a = b + 1, 1 - par, b - 1
                if has(b + 2):
                    ln_factor(b + 2)
                if has(a):
                    pool.wait_ge(gs_ready, a + 1)
                    n = 0

                    def step(ins):
                        nonlocal n
                        n += 1
                        ins.then_inc(gn_ready, 1)
                        wait_apart(pool, gn_ready, 5 * a + n, pool_passed)

                    step(pool.tensor_tensor(gn_m[:], gs[:, :, 0], gs[:, :, 0], ALU.mult))
                    step(pool.tensor_tensor(gn_m[:], gs[:, :, 1], gn_m[:], ALU.subtract))
                    rsqrt_steps(pool, gn_m[:], gn_ve[:], gn_r[:], gn_a[:], gn_chain, RS * a,
                                pool_passed)
                    pool.wait_ge(y_ready, 2 * a)
                    step(pool.tensor_tensor(gn_s[:], gn_r[:], vec[:, V_GA:V_GA + DH], ALU.mult))
                    step(pool.tensor_tensor(gn_m[:], gs[:, :, 0], gn_s[:], ALU.mult))
                    step(pool.tensor_tensor(gn_b[:], vec[:, V_BE:V_BE + DH], gn_m[:], ALU.subtract))
                if has(f):
                    for t in range(TT):
                        wait_apart(pool, v_out, TT * f + t + 1, pool_passed)
                        pool.tensor_tensor(route.score[:, t, bass.ds(f * E, E)], vraw[:, t % 2, D:D + E],
                                           vraw[:, t % 2, D + E:], ALU.add).then_inc(scored, 1)
                        pool.tensor_tensor(v[fp][:, t, :], vraw[:, t % 2, 0:D], bv[:], ALU.add).then_inc(v_ready, 1)
                        wait_apart(pool, v_ready, TT * f + t + 1, pool_passed)
                        for o in range(2):
                            pool.tensor_copy(
                                vm[fp][:, t, o, :].rearrange("p (r a d) -> p r a d", a=2, d=HD)[:, :, o, :],
                                v[fp][:, t, :].rearrange("p (r a d) -> p r a d", a=2, d=HD)[:, :, o, :]
                            ).then_inc(vm_ready, 1)
                if has(f):
                    for h in range(DH):
                        pool.wait_ge(qk32, 4 * f + h + 1)
                        pool.tensor_tensor(qd[fp][:, h, :].rearrange("p (c i) -> p c i", c=TT),
                                           q32[:, h, :].rearrange("p (c i) -> p c i", c=TT),
                                           repeat(qdec, TT), ALU.mult).then_inc(qd_ready, 1)

            passes(pool, one)

        @block.scalar
        def _(act):
            act.wait_ge(consts_in, 16 * 8)
            for i in range(2):
                act.activation(w_hi[i][:], wst[:, i], ACT.Copy).then_inc(w_hi_act, 1)

            def norm(l, par, t):
                if t == 0:
                    act.wait_ge(ln_chain, LS * l + LS)
                    act.wait_ge(xn_stored, 16 * l)
                    act.wait_ge(xnt_ready, 2 * l)
                act.activation(xn[:, t, :], xb[par][:, t, :], ACT.Identity, scale=ln_r[:, t:t + 1],
                               bias=ln_m[:, t:t + 1]).then_inc(xn_ready, 1)

            for t in range(TT):
                norm(0, 0, t)
            act.activation(vg_hi[:, :, 0:D], wst[:, 2], ACT.Copy).then_inc(w_hi_act, 1)

            def one(b, par):
                f, fp, a = b + 1, 1 - par, b - 1
                if has(a):
                    act.wait_ge(av_done, TT * a + TT)
                    for h in range(DH):
                        act.activation(a_hi[:, h, :], ob[h][:], ACT.Copy).then_inc(ahi_ready, 1)
                if has(f):
                    for h in range(DH):
                        act.wait_ge(xnt_ready, 2 * f + h + 1)
                        act.activation(x_hi[:, h, :], fb[h][:], ACT.Copy).then_inc(xhi_ready, 1)
                if has(a):
                    act.wait_ge(yt_mm, 2 * a)
                    for h in range(DH):
                        act.wait_ge(wo_mm, 2 * a + h + 1)
                        act.activation(o32[:, h, :], fb[h][:], ACT.Identity,
                                       bias=vec[:, V_BO + h:V_BO + h + 1]).then_inc(o_ready, 1)
                if has(f):
                    act.wait_ge(qd_ready, 2 * f)
                    for j in range(4):
                        h = j % 2
                        src, hi, bias, of = ((q32, q_hi, V_BQ, C_PAR), (k32, k_hi, V_BK, C_PPAR))[j // 2]
                        act.wait_ge(qk_mm, 4 * f + j + 1)
                        act.activation(src[:, h, :], fb[h][:], ACT.Identity,
                                       bias=vec[:, bias + h:bias + h + 1]).then_inc(qk32, 1)
                        act.wait_ge(qk32, 4 * f + j + 1)
                        act.activation(hi[fp][:, h, 0, :], src[:, h, :], ACT.Copy, scale=parity(0, of))
                        act.activation(hi[fp][:, h, 1, :], src[:, h, :], ACT.Copy,
                                       scale=parity(1, of)).then_inc(qk_hi, 1)
                for t in range(TT):
                    if has(f):
                        act.wait_ge(v_mm, TT * f + t + 1)
                        act.wait_ge(v_ready, least(TT * f + t - 1))
                        act.activation(vraw[:, t % 2, :], fb[t % 2][:, 0:VG], ACT.Copy).then_inc(v_out, 1)
                    if has(b + 2):
                        norm(b + 2, par, t)
                    if t == 1 and has(a):
                        act.wait_ge(gn_ready, 5 * a + 5)
                        for h in range(DH):
                            act.activation(o32[:, h, :], o32[:, h, :], ACT.Identity, scale=gn_s[:, h:h + 1],
                                           bias=gn_b[:, h:h + 1]).then_inc(y_ready, 1)
                if has(f):
                    act.wait_ge(kt_ready, 2 * f + 1)
                    act.activation(kn[fp][:, 0:2, :], fb[0][:].rearrange("p (c d) -> p c d", c=2), ACT.Copy,
                                   scale=kdec).then_inc(kn_ready, 1)
                    act.wait_ge(kt_ready, 2 * f + 2)
                    act.activation(kn[fp][:, 2, :], fb[1][:, 0:D], ACT.Copy, scale=kdec).then_inc(kn_ready, 1)

            passes(act, one)

        @block.vector
        def _(dve):
            def stats(l, k, par):
                dve.wait_ge(x_in[par], 16 * k + 16)
                for t in range(TT):
                    dve.bn_stats(st[:, t, :], xb[par][:, t, :]).then_inc(ln_st, 1)
                wait_apart(dve, ln_st, TT * l + TT, dve_passed)
                for t in range(TT):
                    dve.bn_aggr(mv[:, t, :], st[:, t, :]).then_inc(ln_mv, 1)

            stats(0, 0, 0)
            dve.wait_ge(consts_in, 16 * 8)
            for i in range(4):
                if i < 3:
                    dve.wait_ge(w_hi_act, i + 1)
                else:
                    dve.wait_ge(w_hi_pool, 1)
                hi = vg_hi[:, :, 0:D] if i == 2 else w_hi[i][:]
                dve.tensor_tensor(w_lo[i][:], wst[:, i], hi.bitcast(F32), ALU.subtract).then_inc(w_split, 1)
            dve.wait_ge(w_hi_pool, 2)
            dve.tensor_tensor(vg_hi[:, :, D + E:], gst_w[:], vg_hi[:, :, D:D + E].bitcast(F32),
                              ALU.subtract).then_inc(w_split, 1)

            def state_step(b, c):
                dve.wait_ge(kv_ready, 3 * b + c + 1)
                dve.tensor_tensor(state[c][:], cb[c % 2][:, 0:D].rearrange("p (h d) -> p h d", h=DH),
                                  repeat(bdm, DH), ALU.mult).then_inc(kv_read, 1)
                dve.wait_ge(kv_read, 3 * b + c + 1)
                if c:
                    dve.scalar_tensor_tensor(state[c][:], state[c - 1][:], DECAY ** P, state[c][:],
                                             ALU.mult, ALU.add).then_inc(st_ready, 1)
                    dve.wait_ge(st_ready, 2 * b + c)

            def masked(b, n):
                dve.wait_ge(s_mm, 16 * b + n + 1)
                dve.wait_ge(av_done, least(TT * b + n // PAIRS - 1))
                dve.tensor_tensor(s_sb[n % (2 * PAIRS)][:].rearrange("p h a i -> p (h a) i"),
                                  sbk[n % 2][:].rearrange("p (g i) -> p g i", g=4),
                                  repeat(mask, 4), ALU.mult).then_inc(s_ready, 1)

            def a_split(a, h):
                dve.wait_ge(ahi_ready, 2 * a + h + 1)
                dve.tensor_tensor(a_lo[:, h, :], ob[h][:], a_hi[:, h, :].bitcast(F32),
                                  ALU.subtract).then_inc(alo_ready, 1)

            def x_split(f, h):
                dve.wait_ge(xhi_ready, 2 * f + h + 1)
                dve.tensor_tensor(x_lo[:, h, :], fb[h][:], x_hi[:, h, :].bitcast(F32),
                                  ALU.subtract).then_inc(xlo_ready, 1)

            def qk_split(f, fp, j):
                h = j % 2
                dve.wait_ge(qk_hi, 4 * f + j + 1)
                src, hi, lo, of = ((q32, q_hi, q_lo, C_PAR), (k32, k_hi, k_lo, C_PPAR))[j // 2]
                for o in range(2):
                    last = dve.scalar_tensor_tensor(lo[fp][:, h, o, :], src[:, h, :], parity(o, of),
                                                    hi[fp][:, h, o, :].bitcast(F32), ALU.mult, ALU.subtract)
                last.then_inc(qk_lo, 1)

            def group_moments(a):
                for h in range(DH):
                    dve.wait_ge(o_ready, 2 * a + h + 1)
                    dve.bn_stats(ost[:, h, :], o32[:, h, :]).then_inc(ost_ready, 1)
                wait_apart(dve, ost_ready, 2 * a + 2, dve_passed)
                for h in range(DH):
                    dve.bn_aggr(gm[:, h, :], ost[:, h, :]).then_inc(omv_ready, 1)
                dve.wait_ge(omv_ready, 2 * a + 2)
                for h in range(DH):
                    dve.scalar_tensor_tensor(gm[:, h, 1:2], gm[:, h, 0:1], gm[:, h, 0:1], gm[:, h, 1:2],
                                             ALU.mult, ALU.add).then_inc(gm_ready, 1)

            def residual(a, j):
                dve.wait_ge(res_in, 16 * a + 16)
                dve.wait_ge(yt_mm, 2 * a + j + 1)
                r = res[:, 2 * j:2 * j + 2, :]
                dve.tensor_tensor(r, fb[j][:].rearrange("p (t c) -> p t c", t=2), r,
                                  ALU.add).then_inc(res_ready, 1)

            def one(b, par, k, group=None):
                f, fp, a = b + 1, 1 - par, b - 1
                for n in range(JOBS):
                    if has(b):
                        if n in STATE_AT:
                            state_step(b, STATE_AT.index(n))
                        masked(b, n)
                    if n == 0 and has(a):
                        a_split(a, 0)
                        a_split(a, 1)
                    if n in (1, 2) and has(f):
                        x_split(f, n - 1)
                    if n == STATS_AT and has(b + 2):
                        stats(b + 2, k + 1, par)
                    if n == MOMENTS_AT and has(a):
                        group_moments(a)
                    if n == MEANS_AT + 1 and has(a):
                        dve.wait_ge(gst_mm, a + 1)
                        dve.tensor_copy(gs[:].rearrange("p h s -> p (h s)"), cb[1][:, 0:2 * DH]).then_inc(gs_ready, 1)
                    if 0 <= n - 6 < 4 and has(f):
                        qk_split(f, fp, n - 6)
                    if par and has(b):
                        for m in range(len(SOFTMAX_ODD)):
                            if n == SOFTMAX_ODD[m]:
                                route.softmax_step(dve, k, m, scored)
                    elif not par and has(b - 1):
                        for m in range(len(SOFTMAX_EVEN)):
                            if n == SOFTMAX_EVEN[m]:
                                route.softmax_step(dve, k - 1, len(SOFTMAX_ODD) + m, scored)
                    if group == 0:
                        if n == ROWS_AT and isinstance(b, int) and b == MID:
                            route.take_rows(dve, 0, cb[0])
                        if n == ROUND_AT:
                            route.top_eight(dve, 0, b - MID, par)
                        if n == ROUND_AT + 1:
                            route.their_index(dve, 0, b - MID, par)
                        if n == ROUND_AT + 2:
                            route.strike(dve, 0, b - MID, par)
                    if group == 1:
                        if n == 0:
                            route.as_float(dve, 0)
                        if n == 2:
                            route.take_top(dve, 0, sbk[1])
                        if n == ROWS_AT + 1:
                            route.take_rows(dve, 1, sbk[0])
                            for r in range(Routing.LAST_PASS_ROUNDS // 2):
                                route.whole_round(dve, 1, r)
                    if n in (13, 14) and has(a):
                        residual(a, n - 13)
                    if n == JOBS - 1 and group == 1:
                        for r in range(Routing.LAST_PASS_ROUNDS // 2, Routing.LAST_PASS_ROUNDS):
                            route.whole_round(dve, 1, r)

            MID = Routing.GB
            one(-1, 1, -1)
            one(0, 0, 0)
            one(1, 1, 0)
            with dve.Fori(1, MID // 2) as i:
                one(2 * i, 0, i)
                one(2 * i + 1, 1, i)
            one(MID, 0, MID // 2, group=0)
            one(MID + 1, 1, MID // 2, group=0)
            with dve.Fori(MID // 2 + 1, B // 2 - 2) as i:
                one(2 * i, 0, i, group=0)
                one(2 * i + 1, 1, i, group=0)
            for b in range(B - 4, B):
                one(b, b % 2, b // 2, group=0)
            one(B, 0, B // 2, group=1)

        @block.tensor
        def _(pe):
            pe.wait_ge(consts_in, 16 * 8)

            def product(dst, terms):
                for i, (w, m) in enumerate(terms):
                    last = pe.matmul(dst, w, m, start=i == 0, stop=i == len(terms) - 1)
                return last

            def three(hi, lo, mhi, mlo):
                return [(hi, mhi), (hi, mlo), (lo, mhi)]

            def front(b, f, fp, n):
                h = n % 2
                bank = fb[h]
                if n < 2:
                    pe.wait_ge(xn_ready, TT * f + TT)
                    pe.wait_ge(kn_ready, least(2 * b + h + 1))
                    for t in range(TT):
                        last = pe.transpose(bank[:, t * P:(t + 1) * P], xn[:, t, h * P:(h + 1) * P], ident)
                    last.then_inc(xnt_ready, 1)
                elif 4 <= n < 8:
                    j = n - 4
                    i = j // 2
                    if isinstance(b, int) and b == -1 and j == 0:
                        pe.wait_ge(w_split, 5)
                    pe.wait_ge(xlo_ready, 2 * f + 2)
                    if j < 2:
                        pe.wait_ge(o_ready, least(2 * b - 2 + j + 1))
                    else:
                        pe.wait_ge(qk32, 4 * f + j - 1)
                    cols = slice(h * P, (h + 1) * P)
                    product(bank[:], [p for c in range(DH) for p in
                                      three(w_hi[i][:, c, cols], w_lo[i][:, c, cols],
                                            x_hi[:, c, :], x_lo[:, c, :])]).then_inc(qk_mm, 1)
                elif 8 <= n < 12:
                    t = n - 8
                    if t < 2:
                        pe.wait_ge(qk32, 4 * f + t + 3)
                    else:
                        pe.wait_ge(v_out, TT * f + t - 1)
                    toks = slice(t * P, (t + 1) * P)
                    for c in range(DH):
                        pe.matmul(bank[:, 0:VG], x_hi[:, c, toks], vg_hi[:, c, :], start=c == 0, stop=False,
                                  skip_group_check=True)
                        pe.matmul(bank[:, 0:D], x_hi[:, c, toks], w_lo[2][:, c, :], start=False, stop=False,
                                  skip_group_check=True)
                        last = pe.matmul(bank[:, 0:VG], x_lo[:, c, toks], vg_hi[:, c, :], start=False,
                                         stop=c == DH - 1, skip_group_check=True)
                    last.then_inc(v_mm, 1)
                elif n >= 14:
                    j = n - 14
                    pe.wait_ge(v_out, TT * f + j + 3)
                    pe.wait_ge(res_ready, least(2 * b - 2 + j + 1))
                    for c in (0, 1) if j == 0 else (2,):
                        for g in range(DH):
                            last = pe.transpose(bank[:, (c - 2 * j) * D + g * P:(c - 2 * j) * D + (g + 1) * P],
                                                k32[:, g, c * P:(c + 1) * P], ident)
                    last.then_inc(kt_ready, 1)

            def back(b, a, n):
                j = n % 2
                if 2 <= n < 4:
                    pe.wait_ge(alo_ready, 2 * a + 2)
                    if has(b + 1):
                        pe.wait_ge(xlo_ready, 2 * (b + 1) + j + 1)
                    elif has(b):
                        pe.wait_ge(kn_ready, 2 * b + j + 1)
                    else:
                        pe.wait_ge(res_ready, 2 * b - 3 + j)
                    cols = slice(j * P, (j + 1) * P)
                    product(fb[j][:], [p for c in range(DH) for p in
                                       three(w_hi[3][:, c, cols], w_lo[3][:, c, cols],
                                             a_hi[:, c, :], a_lo[:, c, :])]).then_inc(wo_mm, 1)
                if n == MEANS_AT:
                    pe.wait_ge(gm_ready, 2 * a + 2)
                    pe.wait_ge(kv_read, min(3 * b + 2, 3 * B) if isinstance(b, int) else 3 * b + 2)
                    pe.matmul(cb[1][:, 0:2 * DH], gones, gm[:].rearrange("p h s -> p (h s)"),
                              start=True, stop=True).then_inc(gst_mm, 1)
                if 12 <= n < 14:
                    pe.wait_ge(y_ready, 2 * a + 2)
                    if has(b + 1):
                        pe.wait_ge(v_out, TT * (b + 1) + j + 3)
                    for t in range(2):
                        for h in range(DH):
                            last = pe.transpose(fb[j][:, t * D + h * P:t * D + (h + 1) * P],
                                                o32[:, h, (2 * j + t) * P:(2 * j + t + 1) * P], ident)
                    last.then_inc(yt_mm, 1)

            def scores(b, par, n):
                c, p = n // PAIRS, n % PAIRS
                pe.wait_ge(s_ready, least(16 * b + n - 1))
                rows = slice(64 * (p // 2), 64 * (p // 2) + 64)
                toks = slice(c * P, (c + 1) * P)
                for h in range(DH):
                    last = product(sbk[n % 2][:, h * 2 * P:(h + 1) * 2 * P],
                                   three(k_hi[par][rows, h, p % 2, toks], k_lo[par][rows, h, p % 2, toks],
                                         q_hi[par][rows, h, :, toks], q_lo[par][rows, h, :, toks]))
                last.then_inc(s_mm, 1)

            def chunk_state(b, par, c):
                if c == 0:
                    pe.wait_ge(kn_ready, 2 * b + 2)
                    pe.wait_ge(v_ready, TT * b + TT)
                    pe.wait_ge(kv_read, 3 * b)
                elif c == 1:
                    pe.wait_ge(gs_ready, least(b - 1))
                else:
                    pe.wait_ge(kv_read, 3 * b + 1)
                    if isinstance(b, int) and b == Routing.GB:
                        pe.wait_ge(route.rows_ready, 1)
                for h in range(DH):
                    last = pe.matmul(cb[c % 2][:, h * P:(h + 1) * P], kn[par][:, c, h * P:(h + 1) * P],
                                     v[par][:, c, h * P:(h + 1) * P], start=True, stop=True)
                last.then_inc(kv_ready, 1)

            def values(b, par, c):
                toks = slice(c * P, (c + 1) * P)
                if c == 0:
                    pe.wait_ge(alo_ready, 2 * b)
                else:
                    if c == 1:
                        pe.wait_ge(qd_ready, 2 * b + 2)
                        pe.wait_ge(kv_read, 3 * b + 1)
                    else:
                        pe.wait_ge(st_ready, 2 * b + c - 1)
                    for h in range(DH):
                        pe.matmul(ob[h][:, toks], state[c - 1][:, h, :], qd[par][:, h, toks], start=True, stop=False,
                                  skip_group_check=True)
                pe.wait_ge(vm_ready, 2 * TT * b + 2 * c + 2)
                pe.wait_ge(s_ready, 16 * b + PAIRS * (c + 1))
                for h in range(DH):
                    for a in range(2):
                        for p in range(PAIRS):
                            rows = slice(32 * p, 32 * p + 32)
                            last = pe.matmul(ob[h][rows, toks], vm[par][:, c, a, h * P + 32 * p:h * P + 32 * p + 32],
                                             s_sb[PAIRS * (c % 2) + p][:, h, a, :], start=(c == 0 and a == 0), stop=a == 1,
                                             skip_group_check=True)
                last.then_inc(av_done, 1)

            def one(b, par):
                f, fp, a = b + 1, 1 - par, b - 1
                if has(b):
                    pe.wait_ge(qk_lo, 4 * b + 4)
                for n in range(JOBS):
                    if has(b):
                        for c in range(TT - 1):
                            if n == SUM_AT[c]:
                                chunk_state(b, par, c)
                        scores(b, par, n)
                    if n == 0 and has(a):
                        values(a, 1 - par, TT - 1)
                    if has(b) and n > 1 and n % PAIRS == 1:
                        values(b, par, n // PAIRS - 1)
                    if has(f):
                        front(b, f, fp, n)
                    if has(a):
                        back(b, a, n)
                    if isinstance(b, int) and b == Routing.GB and n == ROWS_AT:
                        pe.wait_ge(kv_read, 3 * b + 1)
                        route.turn_rows(pe, 0, cb[0])
                    if isinstance(b, int) and b == B and n == 1:
                        pe.wait_ge(s_ready, 16 * B)
                        route.turn_top(pe, 0, sbk[1])
                    if isinstance(b, int) and b == B and n == ROWS_AT:
                        route.turn_rows(pe, 1, sbk[0])

            passes(pe, one)


def expert_block(nc, xn_d, out, w1, w2, cst, route, s1, w_in, out_stored):
    with ExitStack() as ctx:
        def sb(name, shape, dt=F32):
            return ctx.enter_context(nc.sbuf_tensor(name, shape, dt))

        def ps(name):
            return ctx.enter_context(nc.psum_tensor(name, [P, 512], F32))

        def sem(name):
            return ctx.enter_context(nc.semaphore(name))

        SL = GRP * CAP
        s2 = sb("w2_stage", [P, FT, D])
        w1h, w1l = ([sb(f"w1_{n}{i}", [P, DH, FF], F32R) for i in range(2)] for n in ("hi", "lo"))
        w2h, w2l = ([sb(f"w2_{n}{i}", [P, FT, D], F32R) for i in range(2)] for n in ("hi", "lo"))
        idx = sb("step_idx", [P, GRP], U32)
        sidx = sb("scatter_idx", [P, GRP], U32)
        xg = [sb(f"xg{i}", [P, D]) for i in range(GRP)]
        xt_hi = sb("xt_hi", [P, DH, SL], F32R)
        xt_lo = sb("xt_lo", [P, DH, SL], F32R)
        g32 = [sb(f"g32_{i}", [P, SL]) for i in range(4)]
        g_hi = sb("g_hi", [P, FT, SL], F32R)
        g_lo = sb("g_lo", [P, FT, SL], F32R)
        y = sb("y", [P, GRP, D])
        tb = [ps("xt0"), ps("xt1")]
        hb = [ps(f"hidden{i}") for i in range(4)]
        yb = [ps("y0"), ps("y1")]

        passed = sem("pool_waits_passed")
        w_hi = sem("w_hi_ready")
        w_lo = sem("w_lo_ready")
        first_hi = sem("first_hi_ready")
        first_lo = sem("first_lo_ready")
        dve_passed = sem("dve_waits_passed")
        route.passed = dve_passed
        idx_ready = sem("idx_ready")
        sidx_ready = sem("sidx_ready")
        gathered = sem("gathered")
        xt_mm = sem("xt_mm")
        xth = sem("xt_hi_ready")
        xtl = sem("xt_lo_ready")
        h_mm = sem("h_mm")
        g_ready = sem("g_ready")
        gh_ready = sem("g_hi_ready")
        gl_ready = sem("g_lo_ready")
        y_mm = sem("y_mm")
        y_ready = sem("y_ready")
        scattered = sem("scattered")
        PIECES = NG

        w1_v = w1.rearrange("e (h p) f -> e p h f", p=P)
        w2_v = w2.rearrange("e (m p) c -> e p m c", p=P)
        out_rows = out.rearrange("b s c -> (b s) c")
        idx_v = route.idxT[:].rearrange("p (b e) -> p b e", e=E)
        p_v = route.pT[:].rearrange("p (b e) -> p b e", e=E)

        def experts(eng, one):
            one(0, 0, True, False)
            one(1, 1, False, False)
            with eng.Fori(1, E // 2 - 1) as i:
                one(2 * i, 0, False, False)
                one(2 * i + 1, 1, False, False)
            one(E - 2, 0, False, False)
            one(E - 1, 1, False, True)

        block = ctx.enter_context(nc.Block())

        @block.sync
        def _(sp):
            def load(e):
                sp.dma_start(s1[:], w1_v[e]).then_inc(w_in, 16)
                sp.dma_start(s2[:], w2_v[e]).then_inc(w_in, 16)

            sp.dma_start(s2[:], w2_v[0]).then_inc(w_in, 16)

            def one(e, par, first, last):
                if not last:
                    if first:
                        sp.wait_ge(first_lo, 4)
                    else:
                        sp.wait_ge(w_lo, PIECES * e)
                    load(e + 1)

            experts(sp, one)

        @block.gpsimd
        def _(pool):
            W = DH * FF // PIECES

            def split(e, par, j):
                last = None
                flat = [(s_[:].rearrange("p a f -> p (a f)"), hi[par][:].rearrange("p a f -> p (a f)"),
                         lo[par][:].rearrange("p a f -> p (a f)")) for s_, hi, lo in ((s1, w1h, w1l), (s2, w2h, w2l))]
                for s_, hi, lo in flat:
                    last = pool.tensor_copy(hi[:, bass.ds(j * W, W)], s_[:, bass.ds(j * W, W)])
                last.then_inc(w_hi, 1)
                wait_apart(pool, w_hi, PIECES * e - PIECES + j + 1, passed)
                for s_, hi, lo in flat:
                    last = pool.tensor_tensor(lo[:, bass.ds(j * W, W)], s_[:, bass.ds(j * W, W)],
                                              hi[:, bass.ds(j * W, W)].bitcast(F32), ALU.subtract)
                last.then_inc(w_lo, 1)

            def take(dst, ready, e, g, n):
                pool.tensor_copy(dst[:].rearrange("p (b o) -> p b o", o=1),
                                 idx_v[:, bass.ds(g * GRP, GRP), bass.ds(e, 1)]).then_inc(ready, 1)
                wait_apart(pool, ready, n + 1, passed)

            def gather(e, g, n):
                wait_apart(pool, gathered, 16 * GRP * n, passed)
                take(idx, idx_ready, e, g, n)
                wait_apart(pool, xt_mm, 2 * n, passed)
                for k in range(GRP):
                    pool.indirect_dma_start(xg[k][:], None, xn_d,
                                            bass.IndirectOffsetOnAxis(idx[:, k:k + 1], 0)).then_inc(gathered, 16)

            def scatter(e, g, n):
                wait_apart(pool, scattered, 16 * GRP * n, passed)
                take(sidx, sidx_ready, e, g, n)
                wait_apart(pool, y_ready, GRP * n + GRP, passed)
                for k in range(GRP):
                    pool.indirect_dma_start(out_rows, bass.IndirectOffsetOnAxis(sidx[:, k:k + 1], 0), y[:, k, :],
                                            None, compute_op=ALU.add).then_inc(scattered, 16)

            gather(0, 0, 0)

            def one(e, par, first, last):
                n0 = NG * e
                gather(e, 1, n0 + 1)
                if first:
                    pool.wait_ge(out_stored, 16 * B)
                else:
                    scatter(e - 1, NG - 1, n0 - 1)
                if not last:
                    wait_apart(pool, w_in, 32 * e + 64, passed)
                    wait_apart(pool, y_mm, GRP * NG * e, passed)
                    split(e + 1, 1 - par, 0)
                if first:
                    for g in range(1, NG // 2 - 1):
                        gather(e, g + 1, g + 1)
                        scatter(e, g - 1, g - 1)
                        split(e + 1, 1 - par, g)
                    pool.wait_ge(route.chosen, 4)
                with pool.Fori(NG // 2 - 1 if first else 1, NG - 1) as g:
                    gather(e, g + 1, n0 + g + 1)
                    scatter(e, g - 1, n0 + g - 1)
                    if not last:
                        split(e + 1, 1 - par, g)
                if not last:
                    gather(e + 1, 0, n0 + NG)
                scatter(e, NG - 2, n0 + NG - 2)
                if not last:
                    split(e + 1, 1 - par, NG - 1)

            experts(pool, one)
            scatter(E - 1, NG - 1, NG * E - 1)
            pool.wait_ge(scattered, 16 * GRP * NG * E)

        @block.scalar
        def _(act):
            def weighted(e, g, n):
                act.wait_ge(scattered, 16 * GRP * n)
                for k in range(GRP):
                    act.wait_ge(y_mm, GRP * n + k + 1)
                    act.activation(y[:, k, :], yb[k % 2][:, 0:D], ACT.Copy,
                                   scale=p_v[:, bass.ds(g * GRP + k, 1), bass.ds(e, 1)].rearrange("p a o -> p (a o)")
                                   ).then_inc(y_ready, 1)

            def transposed(n):
                for h in range(DH):
                    act.wait_ge(xt_mm, 2 * n + h + 1)
                    act.activation(xt_hi[:, h, :], tb[h][:], ACT.Copy).then_inc(xth, 1)

            def hidden(n):
                for m in range(FT):
                    act.wait_ge(h_mm, FT * n + m + 1)
                    act.wait_ge(gl_ready, FT * n + max(m - 3, 0))
                    act.activation(g32[m % 4][:], hb[m % 4][:], ACT.Gelu).then_inc(g_ready, 1)

            for i, (s_, hi) in enumerate(((s1, w1h[0]), (s2, w2h[0]))):
                act.wait_ge(w_in, 16 * i + 16)
                half = s_.shape[1] // 2
                for h in range(2):
                    part = slice(h * half, (h + 1) * half)
                    act.activation(hi[:, part, :], s_[:, part, :], ACT.Copy).then_inc(first_hi, 1)

            def one(e, par, first, last):
                n0 = NG * e
                transposed(n0)
                if not first:
                    weighted(e - 1, NG - 1, n0 - 1)
                hidden(n0)
                with act.Fori(1, NG) as g:
                    transposed(n0 + g)
                    weighted(e, g - 1, n0 + g - 1)
                    hidden(n0 + g)
                if last:
                    weighted(e, NG - 1, n0 + NG - 1)

            experts(act, one)

        @block.vector
        def _(dve):
            k = 0
            for s_, hi, lo in ((s1, w1h[0], w1l[0]), (s2, w2h[0], w2l[0])):
                half = s_.shape[1] // 2
                for h in range(2):
                    part = slice(h * half, (h + 1) * half)
                    k += 1
                    dve.wait_ge(first_hi, k)
                    dve.tensor_tensor(lo[:, part, :], s_[:, part, :], hi[:, part, :].bitcast(F32),
                                      ALU.subtract).then_inc(first_lo, 1)

            def step(n):
                for h in range(DH):
                    dve.wait_ge(xth, 2 * n + h + 1)
                    dve.tensor_tensor(xt_lo[:, h, :], tb[h][:], xt_hi[:, h, :].bitcast(F32),
                                      ALU.subtract).then_inc(xtl, 1)
                if isinstance(n, int) and n > 0:
                    for r in range(Routing.STEP_ROUNDS):
                        route.whole_round(dve, 1, Routing.LAST_PASS_ROUNDS + Routing.STEP_ROUNDS * (n - 1) + r)
                    if n == Routing.LAST_STEP:
                        route.as_float(dve, 1)
                        route.take_top(dve, 1, tb[0])
                for m in range(FT):
                    dve.wait_ge(g_ready, FT * n + m + 1)
                    dve.tensor_copy(g_hi[:, m, :], g32[m % 4][:]).then_inc(gh_ready, 1)
                    dve.wait_ge(gh_ready, FT * n + m + 1)
                    dve.tensor_tensor(g_lo[:, m, :], g32[m % 4][:], g_hi[:, m, :].bitcast(F32),
                                      ALU.subtract).then_inc(gl_ready, 1)

            for n in range(Routing.LAST_STEP + 1):
                step(n)
            with dve.Fori(Routing.LAST_STEP + 1, NG * E) as n:
                step(n)

        @block.tensor
        def _(pe):
            ident = cst[:, C_ID:C_ID + P]

            def transposes(n):
                pe.wait_ge(gathered, 16 * GRP * n + 16 * GRP)
                pe.wait_ge(xtl, 2 * n)
                for h in range(DH):
                    for k in range(GRP):
                        last = pe.transpose(tb[h][:, k * P:(k + 1) * P], xg[k][:, h * P:(h + 1) * P], ident)
                    last.then_inc(xt_mm, 1)

            def up(par, n):
                pe.wait_ge(xtl, 2 * n + 2)
                for m in range(FT):
                    if m >= 4:
                        pe.wait_ge(g_ready, FT * n + m - 3)
                    cols = slice(m * P, (m + 1) * P)
                    i = 0
                    for c in range(DH):
                        for w, x_ in ((w1h, xt_hi), (w1h, xt_lo), (w1l, xt_hi)):
                            last = pe.matmul(hb[m % 4][:], w[par][:, c, cols], x_[:, c, :], start=i == 0,
                                             stop=i == 3 * DH - 1)
                            i += 1
                    last.then_inc(h_mm, 1)

            def down(par, n):
                for k in range(GRP):
                    pe.wait_ge(y_ready, GRP * n + max(k - 1, 0))
                    cols = slice(k * P, (k + 1) * P)
                    i = 0
                    for m in range(FT):
                        if k == 0:
                            pe.wait_ge(gl_ready, FT * n + m + 1)
                        for g_, w in ((g_hi, w2h), (g_hi, w2l), (g_lo, w2h)):
                            last = pe.matmul(yb[k % 2][:, 0:D], g_[:, m, cols], w[par][:, m, :], start=i == 0,
                                             stop=i == 3 * FT - 1)
                            i += 1
                    last.then_inc(y_mm, 1)

            def one(e, par, first, last):
                n0 = NG * e
                transposes(n0)
                if first:
                    pe.wait_ge(first_lo, 2)
                    up(par, n0)
                    pe.wait_ge(first_lo, 4)
                    for n in range(1, NG // 2):
                        transposes(n)
                        down(par, n - 1)
                        if n == Routing.LAST_STEP:
                            pe.wait_ge(xtl, 2 * n + 2)
                            route.turn_top(pe, 1, tb[0])
                        up(par, n)
                else:
                    down(1 - par, n0 - 1)
                    pe.wait_ge(w_lo, PIECES * e)
                    up(par, n0)
                with pe.Fori(NG // 2 if first else 1, NG) as g:
                    transposes(n0 + g)
                    down(par, n0 + g - 1)
                    up(par, n0 + g)
                if last:
                    down(par, n0 + NG - 1)

            experts(pe, one)


def build(nc, x, wq, wk, wv, wo, gw, w1, w2, bvr, cst_d, vec_d, out):
    xn_d = nc.dram_tensor("xn_rows", [B * S, D], F32).ap()
    with ExitStack() as ctx:
        cst = ctx.enter_context(nc.sbuf_tensor("cst", [P, C_N], F32))
        vec = ctx.enter_context(nc.sbuf_tensor("vec", [P, V_N], F32))
        route = Routing(ctx, nc, cst)
        s1 = ctx.enter_context(nc.sbuf_tensor("w1_stage", [P, DH, FF], F32))
        w_in = ctx.enter_context(nc.semaphore("w_in"))
        res = ctx.enter_context(nc.sbuf_tensor("res", [P, TT, D], F32))
        out_stored = ctx.enter_context(nc.semaphore("out_stored"))
        attention_block(nc, x, xn_d, out, wq, wk, wv, wo, gw, w1, bvr, cst_d, vec_d, cst, vec,
                        route, s1, w_in, res, out_stored)
        expert_block(nc, xn_d, out, w1, w2, cst, route, s1, w_in, out_stored)


def constants():
    import numpy as np
    i = np.arange(P)
    c = np.zeros((P, C_N), np.float32)
    c[:, C_ID:C_ID + P] = np.eye(P)
    d = (i[None, :] - i[:, None]).astype(np.float32)
    c[:, C_MASK:C_MASK + P] = np.where(d >= 0, np.exp(d * np.log(DECAY)), 0.0)
    same = (i[None, :] // HD) == (i[:, None] // HD)
    c[:, C_G:C_G + P] = same / HD
    c[:, C_BD:C_BD + P] = same
    c[:, C_QD:C_QD + P] = np.exp((i[None, :] + 1.0) * np.log(DECAY))
    for a in range(2):
        c[:, C_PAR + a] = (i // HD) % 2 == a
        c[:, C_PPAR + a] = (i // (2 * HD)) % 2 == a
    c[:, C_KD] = np.exp((P - 1.0 - i) * np.log(DECAY))
    for g in range(2):
        c[:, C_OFF + g] = (g * (P // E) + i // E) * S
    return c


def kernel(L0_attn_x, L0_attn_Wq, L0_attn_bq, L0_attn_Wk, L0_attn_bk, L0_attn_Wv, L0_attn_bv, L0_attn_Wo,
           L0_attn_bo, L0_attn_gamma, L0_attn_beta, L0_ffn_gate_w, L0_ffn_w1, L0_ffn_w2):
    import numpy as np
    import concourse.bacc as bacc
    from concourse.bass_utils import run_bass_kernel_spmd

    def cols(a):
        return np.asarray(a).reshape(DH, P).T

    vec = np.concatenate([cols(a) for a in (L0_attn_bq, L0_attn_bk, L0_attn_bo, L0_attn_gamma, L0_attn_beta)], 1)
    arrays = {
        "x": L0_attn_x, "wq": L0_attn_Wq, "wk": L0_attn_Wk, "wv": L0_attn_Wv, "wo": L0_attn_Wo,
        "gw": L0_ffn_gate_w, "w1": L0_ffn_w1, "w2": L0_ffn_w2,
        "bvr": np.broadcast_to(np.asarray(L0_attn_bv), (P, D)), "cst": constants(), "vec": vec,
    }
    arrays = {f"in_{n}": np.ascontiguousarray(a) for n, a in arrays.items()}
    nc = bacc.Bacc("TRN2", target_bir_lowering=False, num_devices=1)
    args = [nc.dram_tensor(n, list(a.shape), F32, kind="ExternalInput").ap() for n, a in arrays.items()]
    out = nc.dram_tensor("out", [B, S, D], F32, kind="ExternalOutput").ap()
    build(nc, *args, out)
    r = run_bass_kernel_spmd(nc, [arrays], core_ids=[0])
    return r.results[0]["out"]
```
